# Optimizing a Trainium2 kernel written in Bass

```python
import numpy as np
import jax
import jax.numpy as jnp

def _softmax(x, axis=-1):
    return jax.nn.softmax(x, axis=axis)

def _gelu(x):
    return jax.nn.gelu(x, approximate=True)

def _silu(x):
    return jax.nn.silu(x)

def _sigmoid(x):
    return jax.nn.sigmoid(x)

def _layernorm(x, axis=-1, eps=1e-05):
    m = jnp.mean(x, axis=axis, keepdims=True)
    v = jnp.var(x, axis=axis, keepdims=True)
    return (x - m) / jnp.sqrt(v + eps)

def _scatter_add(tgt, idx, src, axis=0):
    return tgt.at[idx].add(src)

def _segment_sum(src, seg, n):
    return jax.ops.segment_sum(src, seg, n)
kernel_name = 'mk_flamingo_gated_d1_seqx_r8_6d6b5d'

def setup_inputs(seed: int=0):
    np.random.seed(seed)
    _w = jnp.asarray

    def _rec_inputs():
        import jax
        import jax.numpy as jnp
        _rk = jax.random.key(seed)
        x = 7.22e-05 + 1 * jax.random.normal(jax.random.fold_in(_rk, 1), (4, 256, 256), jnp.float32)
        _lenS = 256 - jax.random.randint(jax.random.fold_in(_rk, 7), (4,), 0, max(1, 256 // 4) + 1, jnp.int32)
        _lenS2 = 256 - jax.random.randint(jax.random.fold_in(_rk, 8), (4,), 0, max(1, 256 // 4) + 1, jnp.int32)
        _ctx_1024P = jax.random.normal(jax.random.fold_in(_rk, 11), (4, 16, 128), jnp.float32)
        _ctx_1024c = jax.random.dirichlet(jax.random.fold_in(_rk, 511), 0.3 * jnp.ones((16,), jnp.float32), (4, 256))
        _ctx_1024t = jnp.einsum('bsk,bkd->bsd', _ctx_1024c, _ctx_1024P)
        _ctx_1024t = _ctx_1024t * jax.lax.rsqrt(jnp.mean(jnp.square(_ctx_1024t)) + 1e-12) * 0.953939
        ctx_1024 = 2.81802e-05 + 1.00001 * (_ctx_1024t + 0.3 * jax.random.normal(jax.random.fold_in(_rk, 611), (4, 256, 128), jnp.float32))
        _g = jax.random.normal(jax.random.fold_in(_rk, 9001), (2, 1), jnp.float32)
        _g = jnp.sign(_g) * jnp.maximum(jnp.abs(_g), 1.0) + (_g == 0) * 1.0
        g_xattn = _g[0]
        g_ffn = _g[1]
        return (x, ctx_1024, g_xattn, g_ffn)
    x, ctx_1024, g_xattn, g_ffn = _rec_inputs()

    def _L0_xattn_setup():
        import jax, jax.numpy as jnp
        import numpy as np
        key = jax.random.key(seed)
        ks = jax.random.split(key, 6)
        B, L, N, C, D = (8, 64, 256, 128, 128)
        return {'teacher_logits': jax.random.normal(ks[0], (B, L, N), dtype=jnp.float32), 'teacher_features': jax.random.normal(ks[1], (B, N, C), dtype=jnp.float32), 'Wq': jax.random.normal(ks[2], (D, C), dtype=jnp.float32) * (1.0 / np.sqrt(C)), 'bq': jnp.zeros((D,), dtype=jnp.float32), 'Wk': jax.random.normal(ks[3], (D, C), dtype=jnp.float32) * (1.0 / np.sqrt(C)), 'bk': jnp.zeros((D,), dtype=jnp.float32)}
    _L0_xattn_all = _L0_xattn_setup()
    _L0_xattn_in = {k: v for k, v in _L0_xattn_all.items() if k in ('Wq', 'bq', 'Wk', 'bk')}
    del _L0_xattn_all

    def _L0_ffn_setup():
        import jax, jax.numpy as jnp
        import numpy as np
        TOP_K = 2

        def _gelu(v):
            return jax.nn.gelu(v, approximate=False)
        key = jax.random.key(seed)
        ks = jax.random.split(key, 7)
        B, T, D, I, E = (2, 256, 256, 1024, 8)
        s = 0.02
        return {'x': jax.random.normal(ks[0], (B, T, D), jnp.float32), 'rw1': jax.random.normal(ks[1], (D, D // 2), jnp.float32) * s, 'rw2': jax.random.normal(ks[2], (D // 2, E), jnp.float32) * s, 'w1': jax.random.normal(ks[3], (E, D, I), jnp.float32) * s, 'b1': jax.random.normal(ks[4], (E, I), jnp.float32) * s, 'w2': jax.random.normal(ks[5], (E, I, D), jnp.float32) * s, 'b2': jax.random.normal(ks[6], (E, D), jnp.float32) * s}
    _L0_ffn_all = _L0_ffn_setup()
    _L0_ffn_in = {k: v for k, v in _L0_ffn_all.items() if k in ('rw1', 'rw2', 'w1', 'b1', 'w2', 'b2')}
    del _L0_ffn_all
    return {'x': x, 'ctx_1024': ctx_1024, 'g_xattn': g_xattn, 'g_ffn': g_ffn, 'L0_xattn_Wq': _L0_xattn_in['Wq'], 'L0_xattn_bq': _L0_xattn_in['bq'], 'L0_xattn_Wk': _L0_xattn_in['Wk'], 'L0_xattn_bk': _L0_xattn_in['bk'], 'L0_ffn_rw1': _L0_ffn_in['rw1'], 'L0_ffn_rw2': _L0_ffn_in['rw2'], 'L0_ffn_w1': _L0_ffn_in['w1'], 'L0_ffn_b1': _L0_ffn_in['b1'], 'L0_ffn_w2': _L0_ffn_in['w2'], 'L0_ffn_b2': _L0_ffn_in['b2']}

def reference(x, ctx_1024, g_xattn, g_ffn, L0_xattn_Wq, L0_xattn_bq, L0_xattn_Wk, L0_xattn_bk, L0_ffn_rw1, L0_ffn_rw2, L0_ffn_w1, L0_ffn_b1, L0_ffn_w2, L0_ffn_b2):
    import jax
    import jax.numpy as jnp

    def _L0_xattn_ref(teacher_logits, teacher_features, Wq, bq, Wk, bk):
        import jax, jax.numpy as jnp
        import numpy as np
        query = jnp.einsum('bnc,dc->bnd', teacher_features, Wq) + bq
        key = jnp.einsum('bnc,dc->bnd', teacher_features, Wk) + bk
        energy = jnp.einsum('bnd,bmd->bnm', query, key)
        attention = jax.nn.softmax(energy, axis=-1)
        x_m = jnp.einsum('bln,bmn->blm', teacher_logits, attention)
        return x_m

    def _L0_ffn_ref(x, rw1, rw2, w1, b1, w2, b2):
        import jax, jax.numpy as jnp
        import numpy as np
        TOP_K = 2

        def _gelu(v):
            return jax.nn.gelu(v, approximate=False)
        logits = _gelu(x @ rw1) @ rw2
        probs = jax.nn.softmax(logits, axis=-1)
        wgt, idx = jax.lax.top_k(probs, TOP_K)
        E = w1.shape[0]
        out = jnp.zeros_like(x)
        for e in range(E):
            Ye = _gelu(x @ w1[e] + b1[e]) @ w2[e] + b2[e]
            Ce = _gelu(b1[e]) @ w2[e] + b2[e]
            for k in range(TOP_K):
                mask = idx[..., k] == e
                active = jnp.any(mask).astype(x.dtype)
                term = jnp.where(mask[..., None], Ye, Ce)
                out = out + active * wgt[..., k:k + 1] * term
        return out
    x = x + jnp.tanh(g_xattn[0]) * _L0_xattn_ref(_layernorm(x, axis=-1), ctx_1024, L0_xattn_Wq, L0_xattn_bq, L0_xattn_Wk, L0_xattn_bk)
    x = x + jnp.tanh(g_ffn[0]) * _L0_ffn_ref(_layernorm(x, axis=-1), L0_ffn_rw1, L0_ffn_rw2, L0_ffn_w1, L0_ffn_b1, L0_ffn_w2, L0_ffn_b2)
    return x

_drawn_inputs = setup_inputs


def setup_inputs(seed=0):
    import zlib

    import numpy as np

    out = dict(_drawn_inputs(seed))
    spreads = {'L0_xattn_bq': (0.0, 0.1), 'L0_xattn_bk': (0.0, 0.8)}
    factors = {'L0_ffn_rw1': 4.026,
     'L0_ffn_rw2': 4.023,
     'L0_ffn_w1': 3.576,
     'L0_ffn_b1': 8.0,
     'L0_ffn_w2': 3.378,
     'L0_ffn_b2': 4.822}
    for name, (base, spread) in spreads.items():
        noise = np.random.default_rng([zlib.crc32(name.encode()), seed]).standard_normal(out[name].shape)
        drawn = base * np.exp(spread * noise) if base else spread * noise
        out[name] = jnp.asarray(drawn.astype(out[name].dtype))
    for name, factor in factors.items():
        out[name] = (out[name] * factor).astype(out[name].dtype)
    return out
```

```python
import concourse.bass as bass
from concourse import mybir
from contextlib import ExitStack

P = 128
B, L, D = 4, 256, 256
C = 128
TOK = B * L
T = TOK // P
N_EXP, HID, TOPK = 8, 1024, 2
DC = D // P
HC = HID // P
RH = 128
EPS = 1e-5
BLOCKS = (TOPK * TOK + N_EXP + N_EXP * (P - 1)) // P
ROWS_X = 1 + TOK + N_EXP
ZERO_TOKEN = 1 + TOK
SECOND = 2 * TOK
ROWS_Y = SECOND + TOK + 1
SKIP = 8 * TOK
HALVES = 2 * N_EXP
HW = D * HID // P
RING = 3
BIG = 1e30

C_ID, C_UP, C_IOTA = 0, P, 2 * P
C_DESC = 3 * P
C_LT = C_DESC + N_EXP
C_THR = C_LT + N_EXP * N_EXP
C_BLK = C_THR + N_EXP
C_TOK = C_BLK + BLOCKS
C_DUM = C_TOK + T
C_ALL = C_DUM + 1


def flamingo_moe_kernel(nc, x, ctx_in, g_x, g_f, Wq, bq, Wk, bk, rw1, rw2, w1, b1, w2, b2, consts, out):
    F32, F16, BF16, I32 = mybir.dt.float32, mybir.dt.float16, mybir.dt.bfloat16, mybir.dt.int32
    ALU = mybir.AluOpType
    ACT = mybir.ActivationFunctionType
    X = mybir.AxisListType.X

    ctx = ExitStack()
    with ctx:
        def sb(name, shape, dt):
            return ctx.enter_context(nc.sbuf_tensor(name, shape, dt))

        def sem(name):
            return ctx.enter_context(nc.semaphore(name))

        x_table = nc.dram_tensor("x_table", [ROWS_X, 2 * D], F16, kind="Internal").ap()
        y_table = nc.dram_tensor("y_table", [ROWS_Y, D], F32, kind="Internal").ap()

        w_hi = sb("w_hi", [P, HALVES, HW], F16)
        w_lo = sb("w_lo", [P, HALVES, HW], BF16)
        w1_hi = w_hi[:, :, :].rearrange("p (e j) (d n) -> p e j d n", j=2, d=DC)
        w1_lo = w_lo[:, :, :].rearrange("p (e j) (d n) -> p e j d n", j=2, d=DC)
        w2_hi = w_hi[:, :, :].rearrange("p (e j) (c n) -> p e j c n", j=2, c=HC)
        w2_lo = w_lo[:, :, :].rearrange("p (e j) (c n) -> p e j c n", j=2, c=HC)
        stage = sb("stage", [P, RING, HW], F32)
        y_in = stage[:, :, :].rearrange("p a (b n) -> p (a b) n", n=D)

        cst = sb("cst", [P, C_ALL], F32)
        xs = sb("xs", [P, T, D], F32)
        lnx = sb("lnx", [P, T, D], F32)
        cf = sb("cf", [P, T, C], F32)
        cfT = sb("cfT", [P, TOK], F32)
        qT = sb("qT", [P, TOK], F32)
        kT = sb("kT", [P, TOK], F32)
        split = cfT[:, :].bitcast(F16).rearrange("p (u j n) -> p u j n", u=2, j=2)
        xnT = kT[:, :].rearrange("p (u c n) -> p u c n", u=2, c=2)
        rh = qT[:, 0:2 * L].rearrange("p (u n) -> p u n", u=2)
        prob = sb("prob", [P, 2, 2, L], F32)
        probT = sb("probT", [P, 2, 2, L], F32)
        lnT = sb("lnT", [P, 2, 2, L], F32)
        early = prob[:, :, :, :].rearrange("p a b n -> p (a b n)")
        wqk = early[:, 0:2 * C].rearrange("p (a n) -> p a n", a=2)
        wqkT = early[:, 2 * C:4 * C].rearrange("p (a n) -> p a n", a=2)
        b1r = early[0:HC * N_EXP, 4 * C:4 * C + P]
        rw1_s = sb("rw1_s", [P, DC, RH], F32)
        rw2_s = sb("rw2_s", [P, N_EXP], F32)
        b1T = sb("b1T", [P, HC * N_EXP], F32)
        cb = sb("cb", [2 * N_EXP, D], F32)
        bqk = sb("bqk", [P, 2], F32)
        gate = sb("gate", [P, 2], F32)
        tg = sb("tg", [P, 2], F32)
        bns = sb("bns", [P, T, 6], F32)
        mv = sb("mv", [P, T, 2], F32)
        rstd = sb("rstd", [P, T], F32)
        nmax = sb("nmax", [P, T], F32)
        rsum = sb("rsum", [P, T], F32)
        rinv = sb("rinv", [P, T], F32)
        ident16 = sb("ident16", [P, P], F16)
        identb = sb("identb", [P, P], BF16)
        upper16 = sb("upper16", [P, P], F16)
        ones16 = sb("ones16", [P, P], F16)
        iota16 = sb("iota16", [P, P], F16)
        col0 = sb("col0", [P, P], F16)
        te = [P, T, N_EXP]
        tmp = cf[:, :, :].rearrange("p t n -> p (t n)")
        TE = T * N_EXP
        lg2 = tmp[:, 0:TE].rearrange("p (t e) -> p t e", t=T)
        sc = tmp[:, TE:2 * TE].rearrange("p (t e) -> p t e", t=T)
        slotb = tmp[:, 2 * TE:3 * TE].rearrange("p (t e) -> p t e", t=T)
        sprod = tmp[:, 3 * TE:5 * TE].rearrange("p (k t e) -> p k t e", k=TOPK, t=T)
        dcat = tmp[:, 5 * TE:7 * TE].rearrange("p (k t e) -> p k t e", k=TOPK, t=T)
        ebge = tmp[:, 7 * TE:7 * TE + BLOCKS * N_EXP].rearrange("p (b e) -> p b e", b=BLOCKS)
        lg = sb("lg", te, F32)
        dlg = sb("dlg", te, F32)
        elg = sb("elg", te, F32)
        top = sb("top", [P, TOPK, T], F32)
        pick = sb("pick", [P, TOPK, T], F32)
        E16 = sb("E16", [P, TOPK, T, N_EXP], F16)
        M16 = sb("M16", [P, 2 * T - 1, N_EXP], F16)
        tot = sb("tot", [P, TOPK, N_EXP], F32)
        nexp = sb("nexp", [P, N_EXP], F32)
        ge = sb("ge", [P, N_EXP, N_EXP], F32)
        cnt = sb("cnt", [P, N_EXP], F32)
        st_ = sb("st_", [P, N_EXP], F32)
        en = sb("en", [P, N_EXP], F32)
        sbase = sb("sbase", [P, N_EXP], F32)
        slot = sb("slot", [P, TOPK * T], I32)
        blk_i = sb("blk_i", [P, TOPK * T], I32)
        r_i = sb("r_i", [P, TOPK * T], I32)
        blk_f = sb("blk_f", [P, TOPK * T], F32)
        r_f = sb("r_f", [P, TOPK * T], F32)
        scol = sb("scol", [P, 1], F32)
        dumb = sb("dumb", [P, BLOCKS], F16)
        oh = lnT[:, :, :, :].rearrange("p a b n -> p (a b n)").bitcast(F16)
        ohb = oh[:, 0:TOPK * T * BLOCKS].rearrange("p (k n) -> p k n", n=BLOCKS)
        ohc = oh[:, TOPK * T * BLOCKS:2 * TOPK * T * BLOCKS].rearrange("p (k n) -> p k n", n=BLOCKS)
        ohr = prob[:, :, :, :].rearrange("p a b n -> p (a b n)").bitcast(F16).rearrange(
            "p (k n) -> p k n", n=P)
        ebf = sb("ebf", [P, BLOCKS], F32)
        eb = sb("eb", [P, BLOCKS], I32)
        gidx = sb("gidx", [P, BLOCKS], I32)
        yidx = sb("yidx", [P, BLOCKS], I32)
        yt1 = sb("yt1", [P, BLOCKS], F32)
        yt2 = sb("yt2", [P, BLOCKS], F32)
        gcol = sb("gcol", [P, 2], I32)
        ycol = sb("ycol", [P, 2], I32)
        held = sb("held", [P, 1], F32)
        z = sb("z", [P, T], F32)
        wk = sb("wk", [P, TOPK, T], F32)
        act_f = sb("act_f", [P, TOPK, N_EXP], F32)
        cat = sb("cat", [P, T, 2 * N_EXP], F32)
        catT = kT[0:2 * N_EXP, :]
        xg = probT[:, :, :, :].rearrange("p a b n -> p (a b n)").bitcast(F16).rearrange(
            "p (u n) -> p u n", u=4)
        xT = cfT[:, 0:2 * D].bitcast(F16).rearrange("p (u n) -> p u n", u=2)
        lnx_flat = lnx[:, :, :].rearrange("p t n -> p (t n)")
        hidden = [lnx_flat[:, 0:HID], lnx_flat[:, HID:2 * HID]]
        h_hi = cf[:, :, :].rearrange("p t n -> p (t n)").bitcast(F16).rearrange(
            "p (u c n) -> p u c n", u=2, c=HC)
        h_lo = lnT[:, :, :, :].rearrange("p a b n -> p (a b n)").bitcast(BF16).rearrange(
            "p (u c n) -> p u c n", u=2, c=HC)
        ysb = qT[:, 2 * L:4 * L].rearrange("p (u n) -> p u n", u=2)
        zrow = lnT[0:N_EXP, 0, 0, :].bitcast(F16)

        bank = [ctx.enter_context(nc.psum_tensor(f"bank{i}", [P, 512], F32)) for i in range(8)]

        ident = cst[:, C_ID:C_ID + P]
        desc = cst[:, C_DESC:C_DESC + N_EXP]
        lt = cst[:, C_LT:C_LT + N_EXP * N_EXP].rearrange("p (a b) -> p a b", a=N_EXP)
        thr = cst[:, C_THR:C_THR + N_EXP]
        iota_b = cst[:, C_BLK:C_BLK + BLOCKS]
        tokp1 = cst[:, C_TOK:C_TOK + T]
        dcode = cst[:, C_DUM:C_DUM + 1]

        in_cst, in_ctx, in_wqk, in_x, in_gate = [sem(n) for n in ("in_cst", "in_ctx", "in_wqk", "in_x", "in_gate")]
        in_router, in_bias = sem("in_router"), sem("in_bias")
        in_w = [sem(f"in_w{r}") for r in range(RING)]
        hi_ready, lo_pool, lo_dve = sem("hi_ready"), sem("lo_pool"), sem("lo_dve")
        v_step = sem("v_step")
        small_ready, zero_ready, zero_sent = sem("small_ready"), sem("zero_ready"), sem("zero_sent")
        var_ready, std_ready, ln_ready = sem("var_ready"), sem("std_ready"), sem("ln_ready")
        tg_ready = sem("tg_ready")
        tr_w, tr_ctx = sem("tr_w"), sem("tr_ctx")
        wT_ready, ctxT_a, ctxT_v = sem("wT_ready"), sem("ctxT_a"), sem("ctxT_v")
        q_done, k_done, q_ready, k_ready = sem("q_done"), sem("k_done"), sem("q_ready"), sem("k_ready")
        energy, max_ready, exp_ready, prob_ready = sem("energy"), sem("max_ready"), sem("exp_ready"), sem("prob_ready")
        tr_ln, lnT_ready, tr_p, probT_ready = sem("tr_ln"), sem("lnT_ready"), sem("tr_p"), sem("probT_ready")
        mixed, x2_ready, xn_ready = sem("mixed"), sem("x2_ready"), sem("xn_ready")
        tr_xn, xnT_ready, rh_done, rh_ready, logits = sem("tr_xn"), sem("xnT_ready"), sem("rh_done"), sem("rh_ready"), sem("logits")
        split_ready, table_sent = sem("split_ready"), [sem("table_sent0"), sem("table_sent1")]
        choice_ready, counted, onehot_ready, codes_done, index_ready = [
            sem(n) for n in ("choice_ready", "counted", "onehot_ready", "codes_done", "index_ready")]
        dlg_ready, elg_ready, cat_ready = sem("dlg_ready"), sem("elg_ready"), sem("cat_ready")
        gcol_ready, ycol_ready = sem("gcol_ready"), sem("ycol_ready")
        gathered = [sem("gathered0"), sem("gathered1")]
        scattered = [sem("scattered0"), sem("scattered1")]
        tr_x, xT_ready, h_done, gelu_done, h_ready, y_done, y_ready = [
            sem(n) for n in ("tr_x", "xT_ready", "h_done", "gelu_done", "h_ready", "y_done", "y_ready")]
        tr_cat, catT_ready, in_cb, in_y, const_done, out_ready, out_sent = [
            sem(n) for n in ("tr_cat", "catT_ready", "in_cb", "in_y", "const_done", "out_ready", "out_sent")]

        JN = BLOCKS // 2

        block = ctx.enter_context(nc.Block())

        @block.sync
        def _(sp):
            sp.dma_start(cst[:, :], consts).then_inc(in_cst, 16)
            sp.dma_start(cf[:, :, :], ctx_in.rearrange("b (j p) c -> p (b j) c", p=P)).then_inc(in_ctx, 16)
            sp.dma_start(rw1_s[:, :, :], rw1.rearrange("(d p) n -> p d n", p=P)).then_inc(in_router, 16)
            sp.dma_start(rw2_s[:, :], rw2).then_inc(in_router, 16)
            sp.dma_start(b1r, b1.rearrange("e (c p) -> (e c) p", p=P)).then_inc(in_bias, 16)
            sp.dma_start(cb[N_EXP:2 * N_EXP, :], b2).then_inc(in_bias, 16)

            def weight(h):
                if h >= RING:
                    m = h - RING
                    sp.wait_ge(hi_ready, m + 1)
                    sp.wait_ge(lo_dve if m % 2 else lo_pool, m // 2 + 1)
                e = h // 2
                if h % 2 == 0:
                    src = w1[e].rearrange("(d p) n -> p d n", p=P)
                    dst = stage[:, h % RING, :].rearrange("p (d n) -> p d n", d=DC)
                else:
                    src = w2[e].rearrange("(c p) n -> p c n", p=P)
                    dst = stage[:, h % RING, :].rearrange("p (c n) -> p c n", c=HC)
                sp.dma_start(dst, src).then_inc(in_w[h % RING], 16)

            for h in range(HALVES):
                weight(h)
            for u in range(2):
                sp.wait_ge(scattered[u], 16 * JN)
            sp.dma_start(cb[0:N_EXP, :], y_table[ZERO_TOKEN:ZERO_TOKEN + N_EXP, :]).then_inc(in_cb, 16)
            for half in range(2):
                for k in range(TOPK):
                    r0 = 1 + k * SECOND + half * TOK // 2
                    sp.dma_start(y_in[:, k * T + half * T // 2:k * T + (half + 1) * T // 2, :],
                                 y_table[r0:r0 + TOK // 2, :].rearrange("(t p) n -> p t n", p=P)
                                 ).then_inc(in_y, 16)
                sp.wait_ge(in_y, 32 * (half + 1))
            for q in range(T // 2):
                sp.wait_ge(out_ready, 2 * q + 2)
                sp.dma_start(out.rearrange("b (j p) n -> p (b j) n", p=P)[:, 2 * q:2 * q + 2, :],
                             y_in[:, 2 * q:2 * q + 2, :]).then_inc(out_sent, 16)
            sp.wait_ge(out_sent, 16 * (T // 2))

        @block.gpsimd
        def _(pool):
            for e in range(N_EXP):
                h = 2 * e
                pool.wait_ge(hi_ready, h + 1)
                nc.gpsimd.tensor_tensor(out=w_lo[:, h, :], in0=stage[:, h % RING, :], in1=w_hi[:, h, :],
                                        op=ALU.subtract).then_inc(lo_pool, 1)

            wait = pool.wait_ge

            def hold():
                nc.gpsimd.tensor_tensor(out=held[:, :], in0=cst[:, 0:1], in1=cst[:, 0:1], op=ALU.add)

            def gather(j, u):
                nc.gpsimd.tensor_copy(gcol[:, u:u + 1], gidx[:, bass.ds(2 * j + u, 1)]).then_inc(gcol_ready, 1)
                wait(gcol_ready, 2 * j + u + 1)
                hold()
                nc.gpsimd.indirect_dma_start(
                    out=xg[:, u, :], out_offset=None, in_=x_table,
                    in_offset=bass.IndirectOffsetOnAxis(ap=gcol[:, u:u + 1], axis=0)).then_inc(gathered[u], 16)

            def scatter(j, u):
                wait(y_ready, 2 * j + u + 1)
                nc.gpsimd.tensor_copy(ycol[:, u:u + 1], yidx[:, bass.ds(2 * j + u, 1)]).then_inc(ycol_ready, 1)
                wait(ycol_ready, 2 * j + u + 1)
                hold()
                nc.gpsimd.indirect_dma_start(
                    out=y_table, out_offset=bass.IndirectOffsetOnAxis(ap=ycol[:, u:u + 1], axis=0),
                    in_=ysb[:, u, :], in_offset=None, bounds_check=ROWS_Y - 1,
                    oob_is_err=False).then_inc(scattered[u], 16)

            pool.wait_ge(index_ready, 2)
            pool.wait_ge(in_cst, 16)
            pool.wait_ge(zero_sent, 32)
            for u in range(2):
                pool.wait_ge(table_sent[u], 32)
            for u in range(2):
                gather(0, u)

            def pair(j, first=False, last=False):
                if not last:
                    for u in range(2):
                        wait(tr_x, 2 * j + u + 1)
                        wait(gathered[u], 16 * (j + 1))
                        gather(j + 1, u)
                if not first:
                    if not isinstance(j, int) or j > 1:
                        wait(scattered[1], 16 * (j - 1))
                    scatter(j - 1, 1)
                    wait(scattered[0], 16 * j)
                scatter(j, 0)

            pair(0, first=True)
            pair(1)
            with pool.Fori(2, JN - 1) as j:
                pair(j)
            pair(JN - 1, last=True)
            wait(scattered[1], 16 * (JN - 1))
            scatter(JN - 1, 1)

        @block.scalar
        def _(act):
            x_v = x.rearrange("b (j p) n -> p (b j) n", p=P)
            act.dma_start(wqk[:, 0, :], Wq).then_inc(in_wqk, 16)
            act.dma_start(wqk[:, 1, :], Wk).then_inc(in_wqk, 16)
            act.dma_start(bqk[:, 0:1], bq.rearrange("(p a) -> p a", a=1)).then_inc(in_wqk, 16)
            act.dma_start(bqk[:, 1:2], bk.rearrange("(p a) -> p a", a=1)).then_inc(in_wqk, 16)
            act.dma_start(gate[:, 0:1], g_x.rearrange("(o a) -> o a", a=1).broadcast_to([P, 1])).then_inc(in_gate, 16)
            act.dma_start(gate[:, 1:2], g_f.rearrange("(o a) -> o a", a=1).broadcast_to([P, 1])).then_inc(in_gate, 16)
            act.dma_start(xs[:, :, :], x_v).then_inc(in_x, 16)

            def high(h):
                act.wait_ge(in_w[h % RING], 16 * (h // RING + 1))
                nc.scalar.activation(w_hi[:, h, :], stage[:, h % RING, :], ACT.Copy).then_inc(hi_ready, 1)

            def stds(n):
                act.wait_ge(var_ready, n)
                nc.scalar.activation(rstd[:, :], rstd[:, :], ACT.Sqrt).then_inc(std_ready, 1)

            act.wait_ge(zero_ready, 1)
            act.dma_start(x_table[0:1, :], zrow[0:1, :]).then_inc(zero_sent, 16)
            act.dma_start(x_table[ZERO_TOKEN:ROWS_X, :], zrow).then_inc(zero_sent, 16)
            stds(1)
            act.wait_ge(in_gate, 32)
            nc.scalar.activation(tg[:, :], gate[:, :], ACT.Tanh).then_inc(tg_ready, 1)
            act.wait_ge(tr_ctx, 2)
            nc.scalar.activation(cfT[:, 512:1024], bank[2][:, :], ACT.Copy).then_inc(ctxT_a, 1)
            for h in range(2):
                act.wait_ge(q_done, h + 1)
                nc.scalar.activation(qT[:, 512 * h:512 * h + 512], bank[3 + h][:, :], ACT.Identity,
                                     bias=bqk[:, 0:1]).then_inc(q_ready, 1)
            high(0)
            e_bank = [1, 2, 0, 7]

            def exps(b):
                act.wait_ge(max_ready, b + 1)
                if b >= 2:
                    act.wait_ge(tr_p, b - 1)
                for j in range(2):
                    nc.scalar.activation(prob[:, b % 2, j, :], bank[e_bank[b]][:, L * j:L * j + L], ACT.Exp,
                                         bias=nmax[:, 2 * b + j:2 * b + j + 1],
                                         accum_out=rsum[:, 2 * b + j:2 * b + j + 1]).then_inc(exp_ready, 1)

            def probT_copy(b):
                act.wait_ge(tr_p, b + 1)
                if b >= 2:
                    act.wait_ge(mixed, b - 1)
                nc.scalar.activation(probT[:, b % 2, :, :], bank[e_bank[b]][:, :].rearrange("p (c n) -> p c n", c=2),
                                     ACT.Copy).then_inc(probT_ready, 1)

            exps(0)
            exps(1)
            probT_copy(0)
            exps(2)
            probT_copy(1)
            exps(3)
            high(1)
            probT_copy(2)
            high(2)
            probT_copy(3)
            high(3)
            high(4)
            high(5)
            stds(2)
            for b in range(B):
                act.wait_ge(tr_xn, b + 1)
                if b >= 2:
                    act.wait_ge(rh_done, b - 1)
                nc.scalar.activation(xnT[:, b % 2, :, :], bank[e_bank[b]][:, :].rearrange("p (c n) -> p c n", c=2),
                                     ACT.Copy).then_inc(xnT_ready, 1)
                act.wait_ge(rh_done, b + 1)
                if b >= 2:
                    act.wait_ge(logits, b - 1)
                nc.scalar.activation(rh[:, b % 2, :], bank[3 + b][:, 0:L], ACT.Gelu).then_inc(rh_ready, 1)
            for b in range(B):
                act.wait_ge(split_ready, b + 1)
                act.dma_start(x_table[1 + L * b:1 + L * b + L, :].rearrange("(j p) n -> p j n", p=P),
                              split[:, b % 2, :, :]).then_inc(table_sent[b % 2], 16)
            act.wait_ge(dlg_ready, 1)
            nc.scalar.activation(elg[:, :, :], dlg[:, :, :], ACT.Exp).then_inc(elg_ready, 1)
            for h in range(6, HALVES):
                high(h)

            act.wait_ge(index_ready, 2)

            def gelus(j, u):
                i = 2 * j + u
                e = act.value_load(eb[0:1, bass.ds(i, 1)], min_val=0, max_val=N_EXP - 1)
                if not isinstance(j, int) or j:
                    act.wait_ge(h_ready, 4 * i - 4)
                for half in range(2):
                    act.wait_ge(h_done, 2 * i + half + 1)
                    for c in range(4):
                        cc = 4 * half + c
                        last = nc.scalar.activation(hidden[u][:, cc * P:cc * P + P],
                                                    bank[(0 if u == 0 else 6) + half][:, c * P:c * P + P],
                                                    ACT.Gelu, bias=b1T[:, bass.ds(e * HC + cc, 1)])
                    last.then_inc(gelu_done, 1)

            for u in range(2):
                gelus(0, u)
            with act.Fori(1, JN) as j:
                for u in range(2):
                    gelus(j, u)

        @block.vector
        def _(dve):
            steps = [0]

            def step(ins):
                steps[0] += 1
                ins.then_inc(v_step, 1)
                dve.wait_ge(v_step, steps[0])

            def low(h):
                dve.wait_ge(hi_ready, h + 1)
                nc.vector.tensor_tensor(out=w_lo[:, h, :], in0=stage[:, h % RING, :], in1=w_hi[:, h, :],
                                        op=ALU.subtract).then_inc(lo_dve, 1)

            def variances():
                for t in range(T):
                    last = nc.vector.bn_stats(bns[:, t, :], xs[:, t, :])
                step(last)
                for t in range(T):
                    last = nc.vector.bn_aggr(mv[:, t, :], bns[:, t, :])
                step(last)
                nc.vector.tensor_scalar(rstd[:, :], mv[:, :, 1], EPS, None, ALU.add).then_inc(var_ready, 1)

            def normalise(n, ready):
                dve.wait_ge(std_ready, n)
                step(nc.vector.reciprocal(rstd[:, :], rstd[:, :]))
                for t in range(T):
                    nc.vector.tensor_scalar(lnx[:, t, :], xs[:, t, :], mv[:, t, 0:1], rstd[:, t:t + 1],
                                            ALU.subtract, ALU.mult).then_inc(ready, 1)

            nc.vector.memset(zrow, 0.0).then_inc(zero_ready, 1)
            dve.wait_ge(in_x, 16)
            variances()
            dve.wait_ge(tr_w, 1)
            nc.vector.tensor_copy(wqkT[:, :, :], bank[0][:, 0:2 * C].rearrange("p (a n) -> p a n", a=2)).then_inc(wT_ready, 1)
            dve.wait_ge(tr_ctx, 1)
            nc.vector.tensor_copy(cfT[:, 0:512], bank[1][:, :]).then_inc(ctxT_v, 1)
            nc.vector.tensor_copy(b1T[:, :], bank[0][:, 2 * C:2 * C + HC * N_EXP]).then_inc(wT_ready, 1)
            for h in range(2):
                dve.wait_ge(k_done, h + 1)
                nc.vector.tensor_scalar(kT[:, 512 * h:512 * h + 512], bank[5 + h][:, :], bqk[:, 1:2], None,
                                        ALU.add).then_inc(k_ready, 1)
            normalise(1, ln_ready)
            e_bank = [1, 2, 0, 7]

            def maxima(b):
                dve.wait_ge(energy, b + 1)
                nc.vector.tensor_reduce(out=nmax[:, 2 * b:2 * b + 2],
                                        in_=bank[e_bank[b]][:, :].rearrange("p (j n) -> p j n", j=2),
                                        axis=X, op=ALU.max, negate=True).then_inc(max_ready, 1)

            def probs(b):
                dve.wait_ge(exp_ready, 2 * b + 2)
                step(nc.vector.reciprocal(rinv[:, 2 * b:2 * b + 2], rsum[:, 2 * b:2 * b + 2]))
                for j in range(2):
                    last = nc.vector.tensor_scalar(prob[:, b % 2, j, :], prob[:, b % 2, j, :],
                                                   rinv[:, 2 * b + j:2 * b + j + 1], None, ALU.mult)
                last.then_inc(prob_ready, 1)

            def lnT_copy(b):
                dve.wait_ge(tr_ln, b + 1)
                if b >= 2:
                    dve.wait_ge(mixed, b - 1)
                nc.vector.tensor_copy(lnT[:, b % 2, :, :], bank[3 + b][:, :].rearrange("p (c n) -> p c n", c=2)
                                      ).then_inc(lnT_ready, 1)

            def residual(b):
                dve.wait_ge(mixed, b + 1)
                if b == 0:
                    dve.wait_ge(tg_ready, 1)
                nc.vector.scalar_tensor_tensor(out=xs[:, 2 * b:2 * b + 2, :],
                                               in0=bank[3 + b][:, :].rearrange("p (j n) -> p j n", j=2),
                                               scalar=tg[:, 0:1], in1=xs[:, 2 * b:2 * b + 2, :],
                                               op0=ALU.mult, op1=ALU.add).then_inc(x2_ready, 1)

            maxima(0)
            maxima(1)
            dve.wait_ge(zero_sent, 32)
            lnT_copy(0)
            probs(0)
            maxima(2)
            lnT_copy(1)
            probs(1)
            maxima(3)
            residual(0)
            lnT_copy(2)
            probs(2)
            residual(1)
            lnT_copy(3)
            probs(3)
            nc.vector.tensor_copy(ident16[:, :], ident)
            nc.vector.tensor_copy(identb[:, :], ident)
            nc.vector.tensor_copy(upper16[:, :], cst[:, C_UP:C_UP + P])
            nc.vector.tensor_copy(iota16[:, :], cst[:, C_IOTA:C_IOTA + P])
            nc.vector.memset(ones16[:, :], 1.0)
            nc.vector.memset(M16[:, 0:T - 1, :], 0.0)
            nc.vector.tensor_scalar(col0[:, :], cst[:, C_IOTA:C_IOTA + P], 0.0, None,
                                    ALU.is_equal).then_inc(small_ready, 1)
            residual(2)
            low(1)
            residual(3)
            dve.wait_ge(x2_ready, 4)
            variances()
            normalise(2, xn_ready)
            for b in range(B):
                dve.wait_ge(xn_ready, 2 * b + 2)
                if b >= 2:
                    dve.wait_ge(table_sent[b % 2], 16)
                hi_p, lo_p = split[:, b % 2, :, 0:D], split[:, b % 2, :, D:2 * D].bitcast(BF16)
                step(nc.vector.tensor_copy(hi_p, lnx[:, 2 * b:2 * b + 2, :]))
                nc.vector.tensor_tensor(out=lo_p, in0=lnx[:, 2 * b:2 * b + 2, :], in1=hi_p,
                                        op=ALU.subtract).then_inc(split_ready, 1)
            low(3)

            def e_bc(ap):
                return ap.unsqueeze(1).broadcast_to(te)

            def t_bc(ap):
                return ap.unsqueeze(2).broadcast_to(te)

            dve.wait_ge(logits, B)
            lg_ps = bank[1][:, 0:T * N_EXP].rearrange("p (t e) -> p t e", t=T)
            step(nc.vector.tensor_copy(lg[:, :, :], lg_ps))
            for k in range(TOPK):
                src = lg[:, :, :] if k == 0 else lg2
                step(nc.vector.tensor_reduce(out=top[:, k, :], in_=src, axis=X, op=ALU.max))
                step(nc.vector.tensor_tensor(out=sc, in0=src, in1=t_bc(top[:, k, :]), op=ALU.is_equal))
                step(nc.vector.tensor_tensor(out=sc, in0=sc, in1=e_bc(desc), op=ALU.mult))
                step(nc.vector.tensor_reduce(out=pick[:, k, :], in_=sc, axis=X, op=ALU.max))
                step(nc.vector.tensor_tensor(out=E16[:, k, :, :], in0=e_bc(desc), in1=t_bc(pick[:, k, :]), op=ALU.is_equal))
                if k == 0:
                    step(nc.vector.scalar_tensor_tensor(out=lg2, in0=E16[:, 0, :, :], scalar=-BIG,
                                                        in1=lg[:, :, :], op0=ALU.mult, op1=ALU.add))
            nc.vector.tensor_tensor(out=M16[:, T - 1:2 * T - 1, :], in0=E16[:, 0, :, :], in1=E16[:, 1, :, :],
                                    op=ALU.add).then_inc(choice_ready, 1)
            nc.vector.tensor_tensor(out=dlg[:, :, :], in0=lg[:, :, :], in1=t_bc(top[:, 0, :]),
                                    op=ALU.subtract).then_inc(dlg_ready, 1)
            dve.wait_ge(counted, 1)
            step(nc.vector.tensor_reduce(out=tot[:, :, :],
                                         in_=bank[2][:, P:2 * P].rearrange("p (k t e) -> p k e t", k=TOPK, t=T),
                                         axis=X, op=ALU.add))
            step(nc.vector.tensor_tensor(out=nexp[:, :], in0=tot[:, 0, :], in1=tot[:, 1, :], op=ALU.add))
            ee = [P, N_EXP, N_EXP]
            step(nc.vector.tensor_tensor(out=ge[:, :, :], in0=nexp[:, :].unsqueeze(2).broadcast_to(ee),
                                         in1=thr.unsqueeze(1).broadcast_to(ee), op=ALU.is_ge))
            step(nc.vector.tensor_reduce(out=cnt[:, :], in_=ge[:, :, :], axis=X, op=ALU.add))
            step(nc.vector.tensor_scalar(cnt[:, :], cnt[:, :], 1.0, None, ALU.add))
            step(nc.vector.tensor_tensor(out=ge[:, :, :], in0=lt, in1=cnt[:, :].unsqueeze(1).broadcast_to(ee), op=ALU.mult))
            step(nc.vector.tensor_reduce(out=st_[:, :], in_=ge[:, :, :], axis=X, op=ALU.add))
            step(nc.vector.tensor_scalar(sbase[:, :], st_[:, :], float(P), 1.0, ALU.mult, ALU.add))
            step(nc.vector.tensor_tensor(out=slotb, in0=bank[2][:, 0:T * N_EXP].rearrange("p (t e) -> p t e", t=T),
                                         in1=e_bc(sbase[:, :]), op=ALU.add))
            kte = [P, TOPK, T * N_EXP]
            e2 = E16[:, :, :, :].rearrange("p k t e -> p k (t e)")
            sp2 = sprod.rearrange("p k t e -> p k (t e)")
            step(nc.vector.tensor_tensor(out=sp2, in0=e2,
                                         in1=slotb.rearrange("p t e -> p (t e)").unsqueeze(1).broadcast_to(kte),
                                         op=ALU.mult))
            step(nc.vector.tensor_reduce(out=r_f[:, :], in_=sprod.rearrange("p k t e -> p (k t) e"),
                                         axis=X, op=ALU.add))
            step(nc.vector.tensor_copy(slot[:, :], r_f[:, :]))
            nc.vector.tensor_scalar(blk_i[:, :], slot[:, :], 7, None, ALU.logical_shift_right)
            step(nc.vector.tensor_scalar(r_i[:, :], slot[:, :], P - 1, None, ALU.bitwise_and))
            nc.vector.tensor_copy(blk_f[:, :], blk_i[:, :])
            step(nc.vector.tensor_copy(r_f[:, :], r_i[:, :]))
            kb = [P, TOPK * T, BLOCKS]
            step(nc.vector.tensor_tensor(out=ohb[:, :, :], in0=iota_b.unsqueeze(1).broadcast_to(kb),
                                         in1=blk_f[:, :].unsqueeze(2).broadcast_to(kb), op=ALU.is_equal))
            for k in range(TOPK):
                nc.vector.tensor_tensor(out=ohc[:, k * T:(k + 1) * T, :], in0=ohb[:, k * T:(k + 1) * T, :],
                                        in1=tokp1.unsqueeze(2).broadcast_to([P, T, BLOCKS]), op=ALU.mult)
            step(nc.vector.tensor_tensor(out=ge[:, 0, :], in0=st_[:, :], in1=cst[:, C_ID:C_ID + N_EXP], op=ALU.mult))
            step(nc.vector.tensor_reduce(out=scol[:, :], in_=ge[:, 0, :], axis=X, op=ALU.add))
            nc.vector.tensor_scalar(dumb[:, :], iota_b, scol[:, :], dcode, ALU.is_equal, ALU.mult)
            for kt in range(TOPK * T):
                last = nc.vector.tensor_scalar(ohr[:, kt, :], iota16[:, :], r_f[:, kt:kt + 1], None, ALU.is_equal)
                last.then_inc(onehot_ready, 1)
            step(nc.vector.tensor_tensor(out=en[:, :], in0=st_[:, :], in1=cnt[:, :], op=ALU.add))
            be = [P, BLOCKS, N_EXP]
            step(nc.vector.tensor_tensor(out=ebge, in0=iota_b.unsqueeze(2).broadcast_to(be),
                                         in1=en[:, :].unsqueeze(1).broadcast_to(be), op=ALU.is_ge))
            step(nc.vector.tensor_reduce(out=ebf[:, :], in_=ebge, axis=X, op=ALU.add))
            nc.vector.tensor_scalar(eb[:, :], ebf[:, :], float(N_EXP - 1), None, ALU.min)
            dve.wait_ge(codes_done, 1)
            code = bank[0][:, 0:BLOCKS]
            nc.vector.tensor_copy(gidx[:, :], code).then_inc(index_ready, 1)
            step(nc.vector.tensor_scalar(yt1[:, :], code, 0.0, float(SKIP), ALU.is_equal, ALU.mult))
            step(nc.vector.tensor_tensor(out=yt2[:, :], in0=yt1[:, :], in1=code, op=ALU.add))
            nc.vector.scalar_tensor_tensor(out=yidx[:, :], in0=bank[0][:, BLOCKS:2 * BLOCKS], scalar=float(SECOND),
                                           in1=yt2[:, :], op0=ALU.mult, op1=ALU.add).then_inc(index_ready, 1)

            dve.wait_ge(elg_ready, 1)
            step(nc.vector.tensor_reduce(out=z[:, :], in_=elg[:, :, :], axis=X, op=ALU.add))
            step(nc.vector.reciprocal(z[:, :], z[:, :]))
            step(nc.vector.tensor_tensor(out=sp2, in0=e2,
                                         in1=elg[:, :, :].rearrange("p t e -> p (t e)").unsqueeze(1).broadcast_to(kte),
                                         op=ALU.mult))
            step(nc.vector.tensor_reduce(out=wk[:, :, :], in_=sprod, axis=X, op=ALU.add))
            step(nc.vector.scalar_tensor_tensor(out=wk[:, :, :], in0=wk[:, :, :], scalar=tg[:, 1:2],
                                                in1=z[:, :].unsqueeze(1).broadcast_to([P, TOPK, T]),
                                                op0=ALU.mult, op1=ALU.mult))
            step(nc.vector.tensor_scalar(act_f[:, :, :], tot[:, :, :], 0.0, None, ALU.is_gt))
            for k in range(TOPK):
                step(nc.vector.tensor_tensor(out=dcat[:, k, :, :], in0=e_bc(act_f[:, k, :]), in1=E16[:, k, :, :],
                                             op=ALU.subtract))
                step(nc.vector.tensor_tensor(out=dcat[:, k, :, :], in0=dcat[:, k, :, :], in1=t_bc(wk[:, k, :]),
                                             op=ALU.mult))
                step(nc.vector.tensor_tensor(out=sprod[:, k, :, :], in0=e_bc(act_f[:, k, :]), in1=t_bc(wk[:, k, :]),
                                             op=ALU.mult))
            nc.vector.tensor_tensor(out=cat[:, :, 0:N_EXP], in0=dcat[:, 0, :, :], in1=dcat[:, 1, :, :], op=ALU.add)
            nc.vector.tensor_tensor(out=cat[:, :, N_EXP:2 * N_EXP], in0=sprod[:, 0, :, :], in1=sprod[:, 1, :, :],
                                    op=ALU.add).then_inc(cat_ready, 1)
            for h in range(5, HALVES, 2):
                low(h)

            def xT_copy(j, u):
                i = 2 * j + u
                dve.wait_ge(tr_x, i + 1)
                if not isinstance(j, int) or j:
                    dve.wait_ge(h_done, 2 * i - 2)
                nc.vector.tensor_copy(xT[:, u, :].bitcast(I32),
                                      bank[2 + u][:, 0:D].bitcast(I32)).then_inc(xT_ready, 1)

            def hidden_split(j, u):
                i = 2 * j + u
                if not isinstance(j, int) or j:
                    dve.wait_ge(y_done, i - 1)
                for half in range(2):
                    dve.wait_ge(gelu_done, 2 * i + half + 1)
                    hs = hidden[u][:, 512 * half:512 * half + 512].rearrange("p (c n) -> p c n", n=P)
                    hh, hl = h_hi[:, u, 4 * half:4 * half + 4, :], h_lo[:, u, 4 * half:4 * half + 4, :]
                    nc.vector.tensor_copy(hh, hs).then_inc(h_ready, 1)
                    dve.wait_ge(h_ready, 4 * i + 2 * half + 1)
                    nc.vector.tensor_tensor(out=hl, in0=hs, in1=hh, op=ALU.subtract).then_inc(h_ready, 1)

            def y_copy(j, u):
                i = 2 * j + u
                dve.wait_ge(y_done, i + 1)
                if not isinstance(j, int) or j:
                    dve.wait_ge(scattered[u], 16 * j)
                nc.vector.tensor_copy(ysb[:, u, :], bank[4 + u][:, 0:D]).then_inc(y_ready, 1)

            xT_copy(0, 0)
            xT_copy(0, 1)
            hidden_split(0, 0)
            xT_copy(1, 0)
            hidden_split(0, 1)
            y_copy(0, 0)
            with dve.Fori(1, JN - 1) as j:
                xT_copy(j, 1)
                hidden_split(j, 0)
                y_copy(j - 1, 1)
                xT_copy(j + 1, 0)
                hidden_split(j, 1)
                y_copy(j, 0)
            j = JN - 1
            xT_copy(j, 1)
            hidden_split(j, 0)
            y_copy(j - 1, 1)
            hidden_split(j, 1)
            y_copy(j, 0)
            y_copy(j, 1)

            dve.wait_ge(tr_cat, 1)
            for half in range(2):
                nc.vector.tensor_copy(catT[:, 512 * half:512 * half + 512],
                                      bank[half][0:2 * N_EXP, :]).then_inc(catT_ready, 1)
            for t in range(T):
                if t % (T // 2) == 0:
                    dve.wait_ge(in_y, 32 * (2 * t // T + 1))
                if t % 2 == 0:
                    dve.wait_ge(const_done, t // 2 + 1)
                step(nc.vector.scalar_tensor_tensor(out=y_in[:, t, :], in0=y_in[:, t, :], scalar=wk[:, 0, t:t + 1],
                                                    in1=bank[(6, 7, 2, 3)[t // 2]][:, (t % 2) * D:(t % 2 + 1) * D],
                                                    op0=ALU.mult, op1=ALU.add))
                nc.vector.scalar_tensor_tensor(out=y_in[:, t, :], in0=y_in[:, T + t, :], scalar=wk[:, 1, t:t + 1],
                                               in1=y_in[:, t, :], op0=ALU.mult, op1=ALU.add).then_inc(out_ready, 1)

        @block.tensor
        def _(pe):
            mm, tr = nc.tensor.matmul, nc.tensor.transpose
            e_bank = [1, 2, 0, 7]
            pe.wait_ge(in_cst, 16)
            pe.wait_ge(in_wqk, 64)
            pe.wait_ge(in_bias, 32)
            for a in range(2):
                tr(bank[0][:, C * a:C * a + C], wqk[:, a, :], ident)
            tr(bank[0][:, 2 * C:2 * C + HC * N_EXP], b1r, cst[0:HC * N_EXP, C_ID:C_ID + HC * N_EXP]).then_inc(tr_w, 1)
            pe.wait_ge(in_ctx, 16)
            for h in range(2):
                for t in range(4):
                    last = tr(bank[1 + h][:, P * t:P * t + P], cf[:, 4 * h + t, :], ident)
                last.then_inc(tr_ctx, 1)
            pe.wait_ge(wT_ready, 1)
            for h in range(2):
                if h == 0:
                    pe.wait_ge(ctxT_v, 1)
                else:
                    pe.wait_ge(ctxT_a, 1)
                mm(bank[3 + h][:, :], wqkT[:, 0, :], cfT[:, 512 * h:512 * h + 512], start=True, stop=True).then_inc(q_done, 1)
                mm(bank[5 + h][:, :], wqkT[:, 1, :], cfT[:, 512 * h:512 * h + 512], start=True, stop=True).then_inc(k_done, 1)

            def energies(b):
                pe.wait_ge(q_ready, b // 2 + 1)
                pe.wait_ge(k_ready, b // 2 + 1)
                if b == 2:
                    pe.wait_ge(wT_ready, 2)
                for j in range(2):
                    last = mm(bank[e_bank[b]][:, L * j:L * j + L], qT[:, L * b + P * j:L * b + P * j + P],
                              kT[:, L * b:L * b + L], start=True, stop=True)
                last.then_inc(energy, 1)

            def lnT_tr(b):
                pe.wait_ge(ln_ready, 2 * b + 2)
                pe.wait_ge(q_ready, 2)
                pe.wait_ge(k_ready, 2)
                for c in range(2):
                    for j in range(2):
                        last = tr(bank[3 + b][:, L * c + P * j:L * c + P * j + P], lnx[:, 2 * b + j, P * c:P * c + P], ident)
                last.then_inc(tr_ln, 1)

            def probT_tr(b):
                pe.wait_ge(prob_ready, b + 1)
                for c in range(2):
                    for j in range(2):
                        last = tr(bank[e_bank[b]][:, L * c + P * j:L * c + P * j + P], prob[:, b % 2, j, P * c:P * c + P], ident)
                last.then_inc(tr_p, 1)

            def mix(b):
                pe.wait_ge(lnT_ready, b + 1)
                pe.wait_ge(probT_ready, b + 1)
                for j in range(2):
                    for c in range(2):
                        last = mm(bank[3 + b][:, L * j:L * j + L], lnT[:, b % 2, c, P * j:P * j + P],
                                  probT[:, b % 2, c, :], start=(c == 0), stop=(c == 1))
                last.then_inc(mixed, 1)

            for b in range(B):
                energies(b)
            lnT_tr(0)
            lnT_tr(1)
            probT_tr(0)
            lnT_tr(2)
            mix(0)
            probT_tr(1)
            lnT_tr(3)
            mix(1)
            probT_tr(2)
            mix(2)
            probT_tr(3)
            mix(3)
            pe.wait_ge(in_router, 32)

            def xnT_tr(b):
                pe.wait_ge(xn_ready, 2 * b + 2)
                for c in range(2):
                    for j in range(2):
                        last = tr(bank[e_bank[b]][:, L * c + P * j:L * c + P * j + P], lnx[:, 2 * b + j, P * c:P * c + P], ident)
                last.then_inc(tr_xn, 1)

            def router_hidden(b):
                pe.wait_ge(xnT_ready, b + 1)
                pe.wait_ge(x2_ready, b + 1)
                for c in range(DC):
                    last = mm(bank[3 + b][:, 0:L], rw1_s[:, c, :], xnT[:, b % 2, c, :], start=(c == 0), stop=(c == DC - 1))
                last.then_inc(rh_done, 1)

            def router_logits(b):
                pe.wait_ge(rh_ready, b + 1)
                for j in range(2):
                    t = 2 * b + j
                    last = mm(bank[1][:, t * N_EXP:(t + 1) * N_EXP], rh[:, b % 2, P * j:P * j + P], rw2_s[:, :],
                              start=True, stop=True)
                last.then_inc(logits, 1)

            xnT_tr(0)
            xnT_tr(1)
            router_hidden(0)
            xnT_tr(2)
            router_hidden(1)
            router_logits(0)
            xnT_tr(3)
            router_hidden(2)
            router_logits(1)
            router_hidden(3)
            router_logits(2)
            router_logits(3)

            pe.wait_ge(small_ready, 1)
            pe.wait_ge(choice_ready, 1)
            n = T * N_EXP
            m2 = M16[:, :, :].rearrange("p t e -> p (t e)")
            mm(bank[2][:, P:2 * P], ones16[:, :], E16[:, :, :, :].rearrange("p k t e -> p (k t e)"), start=True, stop=True)
            mm(bank[2][:, 0:n], upper16[:, :], m2[:, (T - 1) * N_EXP:(2 * T - 1) * N_EXP], start=True, stop=False)
            for s in range(1, T):
                last = mm(bank[2][:, 0:n], ones16[:, :], m2[:, (T - 1 - s) * N_EXP:(2 * T - 1 - s) * N_EXP],
                          start=False, stop=(s == T - 1))
            last.then_inc(counted, 1)
            pe.wait_ge(onehot_ready, 1)
            mm(bank[0][:, 0:BLOCKS], col0[:, :], dumb[:, :], start=True, stop=False)
            for kt in range(TOPK * T):
                pe.wait_ge(onehot_ready, kt + 1)
                mm(bank[0][:, 0:BLOCKS], ohr[:, kt, :], ohc[:, kt, :], start=False, stop=(kt == TOPK * T - 1))
            for kt in range(T, TOPK * T):
                last = mm(bank[0][:, BLOCKS:2 * BLOCKS], ohr[:, kt, :], ohb[:, kt, :], start=(kt == T),
                          stop=(kt == TOPK * T - 1))
            last.then_inc(codes_done, 1)
            pe.wait_ge(index_ready, 2)

            def tokens_tr(j, u):
                pe.wait_ge(gathered[u], 16 * (j + 1))
                for c in range(2 * DC):
                    if c < DC:
                        last = tr(bank[2 + u][:, :].bitcast(F16)[:, P * c:P * c + P], xg[:, u, P * c:P * c + P], ident16[:, :])
                    else:
                        last = tr(bank[2 + u][:, :].bitcast(BF16)[:, P * c:P * c + P],
                                  xg[:, u, P * c:P * c + P].bitcast(BF16), identb[:, :])
                last.then_inc(tr_x, 1)

            def up(j, u):
                i = 2 * j + u
                e = pe.value_load(eb[0:1, bass.ds(i, 1)], min_val=0, max_val=N_EXP - 1)
                pe.wait_ge(xT_ready, i + 1)
                xh = xT[:, u, 0:D].rearrange("p (d n) -> p d n", d=DC)
                xl = xT[:, u, D:2 * D].bitcast(BF16).rearrange("p (d n) -> p d n", d=DC)
                for half in range(2):
                    for c in range(4):
                        o = bank[(0 if u == 0 else 6) + half][:, c * P:c * P + P]
                        cs = slice((4 * half + c) * P, (4 * half + c + 1) * P)
                        for d in range(DC):
                            mm(o, w1_hi[:, bass.ds(e, 1), 0, d, cs], xh[:, d, :], start=(d == 0), stop=False)
                            mm(o, w1_hi[:, bass.ds(e, 1), 0, d, cs], xl[:, d, :], start=False, stop=False)
                            last = mm(o, w1_lo[:, bass.ds(e, 1), 0, d, cs], xh[:, d, :], start=False, stop=(d == DC - 1))
                    last.then_inc(h_done, 1)

            def down(j, u):
                i = 2 * j + u
                e = pe.value_load(eb[0:1, bass.ds(i, 1)], min_val=0, max_val=N_EXP - 1)
                o = bank[4 + u][:, 0:D]
                for c in range(HC):
                    if c % 4 == 0:
                        pe.wait_ge(h_ready, 4 * i + 2 * (c // 4) + 2)
                    mm(o, h_hi[:, u, c, :], w2_hi[:, bass.ds(e, 1), 1, c, :], start=(c == 0), stop=False)
                    mm(o, h_hi[:, u, c, :], w2_lo[:, bass.ds(e, 1), 1, c, :], start=False, stop=False)
                    last = mm(o, h_lo[:, u, c, :], w2_hi[:, bass.ds(e, 1), 1, c, :], start=False, stop=(c == HC - 1))
                last.then_inc(y_done, 1)

            tokens_tr(0, 0)
            tokens_tr(0, 1)
            pe.wait_ge(lo_pool, 1)
            pe.wait_ge(lo_dve, 1)
            up(0, 0)
            tokens_tr(1, 0)
            pe.wait_ge(lo_pool, 2)
            pe.wait_ge(lo_dve, 2)
            up(0, 1)
            down(0, 0)
            pe.wait_ge(lo_pool, N_EXP)
            pe.wait_ge(lo_dve, N_EXP)

            def pair(j, last=False):
                tokens_tr(j, 1)
                up(j, 0)
                down(j - 1, 1)
                if not last:
                    tokens_tr(j + 1, 0)
                up(j, 1)
                down(j, 0)

            with pe.Fori(1, JN - 1) as j:
                pair(j)
            pair(JN - 1, last=True)
            down(JN - 1, 1)

            pe.wait_ge(cat_ready, 1)
            pe.wait_ge(gelu_done, 2 * BLOCKS)
            pe.wait_ge(xT_ready, BLOCKS)
            for t in range(T):
                last = tr(bank[t // 4][0:2 * N_EXP, P * (t % 4):P * (t % 4) + P], cat[:, t, :], ident)
            last.then_inc(tr_cat, 1)
            pe.wait_ge(catT_ready, 2)
            pe.wait_ge(in_cb, 16)
            for t in range(T):
                o = bank[(6, 7, 2, 3)[t // 2]][:, (t % 2) * D:(t % 2 + 1) * D]
                mm(o, catT[:, P * t:P * t + P], cb[:, :], start=True, stop=False)
                last = mm(o, ident, xs[:, t, :], start=False, stop=True)
                if t % 2:
                    last.then_inc(const_done, 1)


_INS = ['x', 'ctx_1024', 'g_xattn', 'g_ffn', 'L0_xattn_Wq', 'L0_xattn_bq', 'L0_xattn_Wk', 'L0_xattn_bk',
        'L0_ffn_rw1', 'L0_ffn_rw2', 'L0_ffn_w1', 'L0_ffn_b1', 'L0_ffn_w2', 'L0_ffn_b2']


def shape_constants():
    import numpy as np
    c = np.zeros((P, C_ALL), np.float32)
    p = np.arange(P)
    c[:, C_ID:C_ID + P] = np.eye(P)
    c[:, C_UP:C_UP + P] = p[:, None] < p[None, :]
    c[:, C_IOTA:C_IOTA + P] = p[None, :]
    c[:, C_DESC:C_DESC + N_EXP] = N_EXP - np.arange(N_EXP)
    e = np.arange(N_EXP)
    c[:, C_LT:C_LT + N_EXP * N_EXP] = (e[None, :] < e[:, None]).reshape(-1)
    c[:, C_THR:C_THR + N_EXP] = P * (1 + e)
    c[:, C_BLK:C_BLK + BLOCKS] = np.arange(BLOCKS)
    c[:, C_TOK:C_TOK + T] = 1 + p[:, None] + P * np.arange(T)[None, :]
    c[:N_EXP, C_DUM] = ZERO_TOKEN + e
    return c


def kernel(**inputs):
    import numpy as _np
    import concourse.bacc as _bacc
    from concourse import mybir as _mybir
    from concourse.bass_utils import run_bass_kernel_spmd as _run

    nc = _bacc.Bacc("TRN2", target_bir_lowering=False, num_devices=1)
    arrays, args = {}, []
    for name in _INS:
        a = _np.ascontiguousarray(inputs[name])
        arrays[f"in_{name}"] = a
        args.append(nc.dram_tensor(f"in_{name}", a.shape, _mybir.dt.from_np(a.dtype), kind="ExternalInput").ap())
    a = shape_constants()
    arrays["in_consts"] = a
    args.append(nc.dram_tensor("in_consts", a.shape, _mybir.dt.from_np(a.dtype), kind="ExternalInput").ap())
    args.append(nc.dram_tensor("out_0", (B, L, D), _mybir.dt.float32, kind="ExternalOutput").ap())
    flamingo_moe_kernel(nc, *args)
    r = _run(nc, [arrays], core_ids=[0])
    return r.results[0]["out_0"]
```

```python
import concourse.bass as bass
from concourse import mybir
from contextlib import ExitStack

P = 128
B, L, D = 4, 256, 256
C = 128
TOK = B * L
T = TOK // P
N_EXP, HID, TOPK = 8, 1024, 2
DC = D // P
HC = HID // P
RH = 128
EPS = 1e-5
BLOCKS = (TOPK * TOK + N_EXP + N_EXP * (P - 1)) // P
ROWS_X = 1 + TOK + N_EXP
ZERO_TOKEN = 1 + TOK
SECOND = 2 * TOK
ROWS_Y = SECOND + TOK + 1
SKIP = 8 * TOK
QPE = 4
QUARTERS = QPE * N_EXP
QW = D * HID // P // 2
RING = 6
BIG = 1e30

C_ID, C_UP, C_IOTA = 0, P, 2 * P
C_DESC = 3 * P
C_LT = C_DESC + N_EXP
C_THR = C_LT + N_EXP * N_EXP
C_BLK = C_THR + N_EXP
C_TOK = C_BLK + BLOCKS
C_DUM = C_TOK + T
C_ALL = C_DUM + 1


def flamingo_moe_kernel(nc, x, ctx_in, g_x, g_f, Wq, bq, Wk, bk, rw1, rw2, w1, b1, w2, b2, consts, out):
    F32, F16, BF16, I32 = mybir.dt.float32, mybir.dt.float16, mybir.dt.bfloat16, mybir.dt.int32
    ALU = mybir.AluOpType
    ACT = mybir.ActivationFunctionType
    X = mybir.AxisListType.X

    ctx = ExitStack()
    with ctx:
        def sb(name, shape, dt):
            return ctx.enter_context(nc.sbuf_tensor(name, shape, dt))

        def sem(name):
            return ctx.enter_context(nc.semaphore(name))

        x_table = nc.dram_tensor("x_table", [ROWS_X, 2 * D], F16, kind="Internal").ap()
        y_table = nc.dram_tensor("y_table", [ROWS_Y, D], F32, kind="Internal").ap()

        w_hi = sb("w_hi", [P, QUARTERS, QW], F16)
        w_lo = sb("w_lo", [P, QUARTERS, QW], BF16)
        w1_hi, w1_lo = [w[:, :, :].rearrange("p (e q) n -> p e q n", q=QPE) for w in (w_hi, w_lo)]
        w2_hi, w2_lo = [w[:, :, :].rearrange("p (e j q) (c n) -> p e j (q c) n", j=2, q=2, n=D) for w in (w_hi, w_lo)]
        stage = sb("stage", [P, RING, QW], F32)
        w1_words = [w[:, :, :].bitcast(mybir.dt.int32).rearrange("p (e q) n -> p e (q n)", q=QPE) for w in (w_hi, w_lo)]
        w1f = stage[:, 0:4, :].rearrange("p (u h) n -> p u h n", u=2)
        w1f_hi = [w1f[:, u, 0, :].bitcast(F16).rearrange("p (d n) -> p d n", d=DC) for u in range(2)]
        w1f_lo = [w1f[:, u, 1, :].bitcast(BF16).rearrange("p (d n) -> p d n", d=DC) for u in range(2)]
        y_in = stage[:, :, :].rearrange("p a (b n) -> p (a b) n", n=D)

        cst = sb("cst", [P, C_ALL], F32)
        xs = sb("xs", [P, T, D], F32)
        lnx = sb("lnx", [P, T, D], F32)
        cf = sb("cf", [P, T, C], F32)
        cfT = sb("cfT", [P, TOK], F32)
        qT = sb("qT", [P, TOK], F32)
        kT = sb("kT", [P, TOK], F32)
        prob = sb("prob", [P, 2, 2, L], F32)
        probT = sb("probT", [P, 2, 2, L], F32)
        lnT = sb("lnT", [P, 2, 2, L], F32)
        split = [v[:, :].bitcast(F16).rearrange("p (u j n) -> p u j n", u=2, j=2)[:, u]
                 for v in (cfT, probT[:, :, :, :].rearrange("p a b n -> p (a b n)")) for u in range(2)]
        xnT = kT[:, :].rearrange("p (u c n) -> p u c n", u=2, c=2)
        rh = qT[:, 0:2 * L].rearrange("p (u n) -> p u n", u=2)
        early = prob[:, :, :, :].rearrange("p a b n -> p (a b n)")
        wqk = early[:, 0:2 * C].rearrange("p (a n) -> p a n", a=2)
        wqkT = early[:, 2 * C:4 * C].rearrange("p (a n) -> p a n", a=2)
        b1r = early[0:HC * N_EXP, 4 * C:4 * C + P]
        rw1_s = sb("rw1_s", [P, DC, RH], F32)
        rw2_s = sb("rw2_s", [P, N_EXP], F32)
        b1T = sb("b1T", [P, HC * N_EXP], F32)
        cb = sb("cb", [2 * N_EXP, D], F32)
        bqk = sb("bqk", [P, 2], F32)
        gate = sb("gate", [P, 2], F32)
        tg = sb("tg", [P, 2], F32)
        bns = sb("bns", [P, T, 6], F32)
        mv = sb("mv", [P, T, 2], F32)
        rstd = sb("rstd", [P, T], F32)
        nmax = sb("nmax", [P, T], F32)
        rsum = sb("rsum", [P, T], F32)
        rinv = sb("rinv", [P, T], F32)
        ident16 = sb("ident16", [P, P], F16)
        identb = sb("identb", [P, P], BF16)
        upper16 = sb("upper16", [P, P], F16)
        ones16 = sb("ones16", [P, P], F16)
        iota16 = sb("iota16", [P, P], F16)
        col0 = sb("col0", [P, P], F16)
        te = [P, T, N_EXP]
        tmp = cf[:, :, :].rearrange("p t n -> p (t n)")
        TE = T * N_EXP
        lg2 = tmp[:, 0:TE].rearrange("p (t e) -> p t e", t=T)
        sc = tmp[:, TE:2 * TE].rearrange("p (t e) -> p t e", t=T)
        slotb = tmp[:, 2 * TE:3 * TE].rearrange("p (t e) -> p t e", t=T)
        sprod = tmp[:, 3 * TE:5 * TE].rearrange("p (k t e) -> p k t e", k=TOPK, t=T)
        dcat = tmp[:, 5 * TE:7 * TE].rearrange("p (k t e) -> p k t e", k=TOPK, t=T)
        ebge = tmp[:, 7 * TE:7 * TE + BLOCKS * N_EXP].rearrange("p (b e) -> p b e", b=BLOCKS)
        lg = sb("lg", te, F32)
        dlg = sb("dlg", te, F32)
        elg = sb("elg", te, F32)
        top = sb("top", [P, TOPK, T], F32)
        pick = sb("pick", [P, TOPK, T], F32)
        E16 = sb("E16", [P, TOPK, T, N_EXP], F16)
        M16 = sb("M16", [P, 2 * T - 1, N_EXP], F16)
        tot = sb("tot", [P, TOPK, N_EXP], F32)
        nexp = sb("nexp", [P, N_EXP], F32)
        ge = sb("ge", [P, N_EXP, N_EXP], F32)
        cnt = sb("cnt", [P, N_EXP], F32)
        st_ = sb("st_", [P, N_EXP], F32)
        en = sb("en", [P, N_EXP], F32)
        sbase = sb("sbase", [P, N_EXP], F32)
        slot = sb("slot", [P, TOPK * T], I32)
        blk_i = sb("blk_i", [P, TOPK * T], I32)
        r_i = sb("r_i", [P, TOPK * T], I32)
        blk_f = sb("blk_f", [P, TOPK * T], F32)
        r_f = sb("r_f", [P, TOPK * T], F32)
        scol = sb("scol", [P, 1], F32)
        dumb = sb("dumb", [P, BLOCKS], F16)
        oh = lnT[:, :, :, :].rearrange("p a b n -> p (a b n)").bitcast(F16)
        ohb = oh[:, 0:TOPK * T * BLOCKS].rearrange("p (k n) -> p k n", n=BLOCKS)
        ohc = oh[:, TOPK * T * BLOCKS:2 * TOPK * T * BLOCKS].rearrange("p (k n) -> p k n", n=BLOCKS)
        ohr = prob[:, :, :, :].rearrange("p a b n -> p (a b n)").bitcast(F16).rearrange(
            "p (k n) -> p k n", n=P)
        ebf = sb("ebf", [P, BLOCKS], F32)
        eb = sb("eb", [P, BLOCKS], I32)
        gidx = sb("gidx", [P, BLOCKS], I32)
        yidx = sb("yidx", [P, BLOCKS], I32)
        yt1 = sb("yt1", [P, BLOCKS], F32)
        yt2 = sb("yt2", [P, BLOCKS], F32)
        gcol = sb("gcol", [P, 2], I32)
        ycol = sb("ycol", [P, 2], I32)
        held = sb("held", [P, 1], F32)
        warm = sb("warm", [P, 1], F32)
        z = sb("z", [P, T], F32)
        wk = sb("wk", [P, TOPK, T], F32)
        act_f = sb("act_f", [P, TOPK, N_EXP], F32)
        cat = sb("cat", [P, T, 2 * N_EXP], F32)
        catT = kT[0:2 * N_EXP, :]
        xg = probT[:, :, :, :].rearrange("p a b n -> p (a b n)").bitcast(F16).rearrange(
            "p (u n) -> p u n", u=4)
        xT = cfT[:, 0:2 * D].bitcast(F16).rearrange("p (u n) -> p u n", u=2)
        lnx_flat = lnx[:, :, :].rearrange("p t n -> p (t n)")
        hidden = [lnx_flat[:, 0:HID], lnx_flat[:, HID:2 * HID]]
        h_hi = cf[:, :, :].rearrange("p t n -> p (t n)").bitcast(F16).rearrange(
            "p (u c n) -> p u c n", u=2, c=HC)
        h_lo = lnT[:, :, :, :].rearrange("p a b n -> p (a b n)").bitcast(BF16).rearrange(
            "p (u c n) -> p u c n", u=2, c=HC)
        ysb = qT[:, 2 * L:4 * L].rearrange("p (u n) -> p u n", u=2)
        zrow = lnT[0:N_EXP, 0, 0, :].bitcast(F16)

        bank = [ctx.enter_context(nc.psum_tensor(f"bank{i}", [P, 512], F32)) for i in range(8)]

        ident = cst[:, C_ID:C_ID + P]
        desc = cst[:, C_DESC:C_DESC + N_EXP]
        lt = cst[:, C_LT:C_LT + N_EXP * N_EXP].rearrange("p (a b) -> p a b", a=N_EXP)
        thr = cst[:, C_THR:C_THR + N_EXP]
        iota_b = cst[:, C_BLK:C_BLK + BLOCKS]
        tokp1 = cst[:, C_TOK:C_TOK + T]
        dcode = cst[:, C_DUM:C_DUM + 1]

        in_cst, in_ctx, in_wqk, in_x, in_gate = [sem(n) for n in ("in_cst", "in_ctx", "in_wqk", "in_x", "in_gate")]
        in_router, in_bias = sem("in_router"), sem("in_bias")
        in_w = [sem(f"in_w{r}") for r in range(RING)]
        hi_ready, lo_pool, lo_dve = sem("hi_ready"), sem("lo_pool"), sem("lo_dve")
        v_step = sem("v_step")
        small_ready, zero_ready, zero_sent = sem("small_ready"), sem("zero_ready"), sem("zero_sent")
        var_ready, std_ready, ln_ready = sem("var_ready"), sem("std_ready"), sem("ln_ready")
        tg_ready = sem("tg_ready")
        tr_w, tr_ctx = sem("tr_w"), sem("tr_ctx")
        wT_ready, ctxT_a, ctxT_v = sem("wT_ready"), sem("ctxT_a"), sem("ctxT_v")
        q_done, k_done, q_ready, k_ready = sem("q_done"), sem("k_done"), sem("q_ready"), sem("k_ready")
        energy, max_ready, exp_ready, prob_ready = sem("energy"), sem("max_ready"), sem("exp_ready"), sem("prob_ready")
        tr_ln, lnT_ready, tr_p, probT_ready = sem("tr_ln"), sem("lnT_ready"), sem("tr_p"), sem("probT_ready")
        mixed, x2_ready, xn_ready = sem("mixed"), sem("x2_ready"), sem("xn_ready")
        tr_xn, xnT_ready, rh_done, rh_ready, logits = sem("tr_xn"), sem("xnT_ready"), sem("rh_done"), sem("rh_ready"), sem("logits")
        split_ready, table_sent = sem("split_ready"), [sem("table_sent0"), sem("table_sent1")]
        choice_ready, counted, onehot_ready, codes_done, index_ready = [
            sem(n) for n in ("choice_ready", "counted", "onehot_ready", "codes_done", "index_ready")]
        dlg_ready, elg_ready = sem("dlg_ready"), sem("elg_ready")
        w1_fetched = sem("w1_fetched")
        gcol_ready, ycol_ready = sem("gcol_ready"), sem("ycol_ready")
        gathered = [sem("gathered0"), sem("gathered1")]
        scattered = [sem("scattered0"), sem("scattered1")]
        tr_x, xT_ready, h_done, gelu_done, h_ready, y_done, y_ready = [
            sem(n) for n in ("tr_x", "xT_ready", "h_done", "gelu_done", "h_ready", "y_done", "y_ready")]
        tr_cat, catT_ready, in_cb, const_done, out_ready, out_sent = [
            sem(n) for n in ("tr_cat", "catT_ready", "in_cb", "const_done", "out_ready", "out_sent")]
        in_y = [sem(f"in_y{q}") for q in range(T // 2)]

        def by_dve(q):
            return q % QPE == QPE - 1

        def low_done(q):
            mine = [k for k in range(q + 1) if by_dve(k) == by_dve(q)]
            return (lo_dve if by_dve(q) else lo_pool), len(mine)

        JN = BLOCKS // 2

        block = ctx.enter_context(nc.Block())

        @block.sync
        def _(sp):
            sp.dma_start(cst[:, :], consts).then_inc(in_cst, 16)
            sp.dma_start(cf[:, :, :], ctx_in.rearrange("b (j p) c -> p (b j) c", p=P)).then_inc(in_ctx, 16)
            sp.dma_start(xs[:, :, :], x.rearrange("b (j p) n -> p (b j) n", p=P)).then_inc(in_x, 16)
            sp.dma_start(rw1_s[:, :, :], rw1.rearrange("(d p) n -> p d n", p=P)).then_inc(in_router, 16)
            sp.dma_start(rw2_s[:, :], rw2).then_inc(in_router, 16)
            sp.dma_start(b1r, b1.rearrange("e (c p) -> (e c) p", p=P)).then_inc(in_bias, 16)
            sp.dma_start(cb[N_EXP:2 * N_EXP, :], b2).then_inc(in_bias, 16)

            for q in range(QUARTERS):
                if q >= RING:
                    sp.wait_ge(hi_ready, q - RING + 1)
                    sp.wait_ge(*low_done(q - RING))
                e, half = q // QPE, q % 2
                if q % QPE < 2:
                    src = w1[e, P * half:P * half + P, :]
                    dst = stage[:, q % RING, :]
                else:
                    src = w2[e, HID // 2 * half:HID // 2 * (half + 1), :].rearrange("(c p) n -> p c n", p=P)
                    dst = stage[:, q % RING, :].rearrange("p (c n) -> p c n", n=D)
                sp.dma_start(dst, src).then_inc(in_w[q % RING], 16)
            for u in range(2):
                sp.wait_ge(scattered[u], 16 * JN)
            sp.dma_start(cb[0:N_EXP, :], y_table[ZERO_TOKEN:ZERO_TOKEN + N_EXP, :]).then_inc(in_cb, 16)
            for q in range(T // 2):
                for k in range(TOPK):
                    r0 = 1 + k * SECOND + 2 * q * P
                    sp.dma_start(y_in[:, k * T + 2 * q:k * T + 2 * q + 2, :],
                                 y_table[r0:r0 + 2 * P, :].rearrange("(t p) n -> p t n", p=P)
                                 ).then_inc(in_y[q], 16)
            for q in range(T // 2):
                sp.wait_ge(out_ready, 2 * q + 2)
                sp.dma_start(out.rearrange("b (j p) n -> p (b j) n", p=P)[:, 2 * q:2 * q + 2, :],
                             y_in[:, 2 * q:2 * q + 2, :]).then_inc(out_sent, 16)
            sp.wait_ge(out_sent, 16 * (T // 2))

        @block.gpsimd
        def _(pool):
            def lows(a, b):
                for q in range(a, b):
                    if by_dve(q):
                        continue
                    pool.wait_ge(hi_ready, q + 1)
                    nc.gpsimd.tensor_tensor(out=w_lo[:, q, :], in0=stage[:, q % RING, :], in1=w_hi[:, q, :],
                                            op=ALU.subtract).then_inc(lo_pool, 1)

            wait = pool.wait_ge

            def hold():
                nc.gpsimd.tensor_tensor(out=held[:, :], in0=cst[:, 0:1], in1=cst[:, 0:1], op=ALU.add)

            def gather(j, u):
                nc.gpsimd.tensor_copy(gcol[:, u:u + 1], gidx[:, bass.ds(2 * j + u, 1)]).then_inc(gcol_ready, 1)
                wait(gcol_ready, 2 * j + u + 1)
                hold()
                nc.gpsimd.indirect_dma_start(
                    out=xg[:, u, :], out_offset=None, in_=x_table,
                    in_offset=bass.IndirectOffsetOnAxis(ap=gcol[:, u:u + 1], axis=0)).then_inc(gathered[u], 16)

            def scatter(j, u):
                nc.gpsimd.tensor_copy(ycol[:, u:u + 1], yidx[:, bass.ds(2 * j + u, 1)]).then_inc(ycol_ready, 1)
                wait(ycol_ready, 2 * j + u + 1)
                wait(y_ready, 2 * j + u + 1)
                hold()
                nc.gpsimd.indirect_dma_start(
                    out=y_table, out_offset=bass.IndirectOffsetOnAxis(ap=ycol[:, u:u + 1], axis=0),
                    in_=ysb[:, u, :], in_offset=None, bounds_check=ROWS_Y - 1,
                    oob_is_err=False).then_inc(scattered[u], 16)

            lows(0, QUARTERS - QPE)
            pool.wait_ge(index_ready, 1)
            pool.wait_ge(in_cst, 16)
            pool.wait_ge(zero_sent, 32)
            for u in range(2):
                pool.wait_ge(table_sent[u], 32)
            for u in range(2):
                gather(0, u)
            lows(QUARTERS - QPE, QUARTERS)

            def pair(j, first=False, last=False):
                if not last:
                    for u in range(2):
                        wait(tr_x, 2 * j + u + 1)
                        wait(gathered[u], 16 * (j + 1))
                        gather(j + 1, u)
                if first:
                    wait(index_ready, 2)
                else:
                    if not isinstance(j, int) or j > 1:
                        wait(scattered[1], 16 * (j - 1))
                    scatter(j - 1, 1)
                    wait(scattered[0], 16 * j)
                scatter(j, 0)

            pair(0, first=True)
            pair(1)
            with pool.Fori(2, JN - 1) as j:
                pair(j)
            pair(JN - 1, last=True)
            wait(scattered[1], 16 * (JN - 1))
            scatter(JN - 1, 1)

        @block.scalar
        def _(act):
            act.dma_start(wqk[:, 0, :], Wq).then_inc(in_wqk, 16)
            act.dma_start(wqk[:, 1, :], Wk).then_inc(in_wqk, 16)
            act.dma_start(bqk[:, 0:1], bq.rearrange("(p a) -> p a", a=1)).then_inc(in_wqk, 16)
            act.dma_start(bqk[:, 1:2], bk.rearrange("(p a) -> p a", a=1)).then_inc(in_wqk, 16)
            act.dma_start(gate[:, 0:1], g_x.rearrange("(o a) -> o a", a=1).broadcast_to([P, 1])).then_inc(in_gate, 16)
            act.dma_start(gate[:, 1:2], g_f.rearrange("(o a) -> o a", a=1).broadcast_to([P, 1])).then_inc(in_gate, 16)

            def high(a, b):
                for q in range(a, b):
                    act.wait_ge(in_w[q % RING], 16 * (q // RING + 1))
                    nc.scalar.activation(w_hi[:, q, :], stage[:, q % RING, :], ACT.Copy).then_inc(hi_ready, 1)

            def stds(n):
                act.wait_ge(var_ready, n)
                nc.scalar.activation(rstd[:, :], rstd[:, :], ACT.Sqrt).then_inc(std_ready, 1)

            act.wait_ge(zero_ready, 1)
            act.dma_start(x_table[0:1, :], zrow[0:1, :]).then_inc(zero_sent, 16)
            act.dma_start(x_table[ZERO_TOKEN:ROWS_X, :], zrow).then_inc(zero_sent, 16)
            stds(1)
            high(0, 1)
            act.wait_ge(tr_ctx, 2)
            nc.scalar.activation(cfT[:, 512:1024], bank[2][:, :], ACT.Copy).then_inc(ctxT_a, 1)
            high(1, 2)
            for h in range(2):
                act.wait_ge(q_done, h + 1)
                nc.scalar.activation(qT[:, 512 * h:512 * h + 512], bank[3 + h][:, :], ACT.Identity,
                                     bias=bqk[:, 0:1]).then_inc(q_ready, 1)
                if h == 0:
                    high(2, 4)
            act.wait_ge(in_gate, 32)
            nc.scalar.activation(tg[:, :], gate[:, :], ACT.Tanh).then_inc(tg_ready, 1)
            high(4, 6)
            e_bank = [1, 2, 0, 7]

            def exps(b):
                act.wait_ge(max_ready, b + 1)
                if b >= 2:
                    act.wait_ge(tr_p, b - 1)
                for j in range(2):
                    nc.scalar.activation(prob[:, b % 2, j, :], bank[e_bank[b]][:, L * j:L * j + L], ACT.Exp,
                                         bias=nmax[:, 2 * b + j:2 * b + j + 1],
                                         accum_out=rsum[:, 2 * b + j:2 * b + j + 1]).then_inc(exp_ready, 1)

            def probT_copy(b):
                act.wait_ge(tr_p, b + 1)
                if b >= 2:
                    act.wait_ge(mixed, b - 1)
                nc.scalar.activation(probT[:, b % 2, :, :], bank[e_bank[b]][:, :].rearrange("p (c n) -> p c n", c=2),
                                     ACT.Copy).then_inc(probT_ready, 1)

            exps(0)
            exps(1)
            high(6, 7)
            probT_copy(0)
            exps(2)
            high(7, 9)
            probT_copy(1)
            exps(3)
            high(9, 11)
            probT_copy(2)
            high(11, 13)
            probT_copy(3)
            high(13, 15)
            stds(2)
            high(15, 17)

            def xnT_copy(b):
                act.wait_ge(tr_xn, b + 1)
                if b >= 2:
                    act.wait_ge(rh_done, b - 1)
                nc.scalar.activation(xnT[:, b % 2, :, :], bank[e_bank[b]][:, :].rearrange("p (c n) -> p c n", c=2),
                                     ACT.Copy).then_inc(xnT_ready, 1)

            def router_gelu(b):
                act.wait_ge(rh_done, b + 1)
                if b >= 2:
                    act.wait_ge(logits, b - 1)
                nc.scalar.activation(rh[:, b % 2, :], bank[3 + b][:, 0:L], ACT.Gelu).then_inc(rh_ready, 1)

            def send(b):
                act.wait_ge(split_ready, b + 1)
                act.dma_start(x_table[1 + L * b:1 + L * b + L, :].rearrange("(j p) n -> p j n", p=P),
                              split[b][:, :, :]).then_inc(table_sent[b % 2], 16)

            xnT_copy(0)
            xnT_copy(1)
            router_gelu(0)
            high(17, 18)
            xnT_copy(2)
            router_gelu(1)
            high(18, 19)
            xnT_copy(3)
            router_gelu(2)
            send(0)
            send(1)
            high(19, 20)
            router_gelu(3)
            send(2)
            send(3)
            high(20, QUARTERS)
            act.wait_ge(dlg_ready, 1)
            nc.scalar.activation(elg[:, :, :], dlg[:, :, :], ACT.Exp).then_inc(elg_ready, 1)
            nc.scalar.activation(warm[:, :], tg[:, 0:1], ACT.Gelu)

            act.wait_ge(index_ready, 1)

            def gelus(j, u):
                i = 2 * j + u
                e = act.value_load(eb[0:1, bass.ds(i, 1)], min_val=0, max_val=N_EXP - 1)
                if not isinstance(j, int) or j:
                    act.wait_ge(h_ready, 4 * i - 4)
                for half in range(2):
                    act.wait_ge(h_done, 2 * i + half + 1)
                    for c in range(4):
                        cc = 4 * half + c
                        last = nc.scalar.activation(hidden[u][:, cc * P:cc * P + P],
                                                    bank[(0 if u == 0 else 6) + half][:, c * P:c * P + P],
                                                    ACT.Gelu, bias=b1T[:, bass.ds(e * HC + cc, 1)])
                    last.then_inc(gelu_done, 1)

            for u in range(2):
                gelus(0, u)
            with act.Fori(1, JN) as j:
                for u in range(2):
                    gelus(j, u)

        @block.vector
        def _(dve):
            steps = [0]

            def step(ins):
                steps[0] += 1
                ins.then_inc(v_step, 1)
                dve.wait_ge(v_step, steps[0])

            def low(q):
                dve.wait_ge(hi_ready, q + 1)
                nc.vector.tensor_tensor(out=w_lo[:, q, :], in0=stage[:, q % RING, :], in1=w_hi[:, q, :],
                                        op=ALU.subtract).then_inc(lo_dve, 1)

            def stats(t0, t1):
                for t in range(t0, t1):
                    last = nc.vector.bn_stats(bns[:, t, :], xs[:, t, :])
                return last

            def variances(last):
                step(last)
                for t in range(T):
                    last = nc.vector.bn_aggr(mv[:, t, :], bns[:, t, :])
                step(last)
                nc.vector.tensor_scalar(rstd[:, :], mv[:, :, 1], EPS, None, ALU.add).then_inc(var_ready, 1)

            def normalise(n, ready):
                dve.wait_ge(std_ready, n)
                step(nc.vector.reciprocal(rstd[:, :], rstd[:, :]))
                for t in range(T):
                    nc.vector.tensor_scalar(lnx[:, t, :], xs[:, t, :], mv[:, t, 0:1], rstd[:, t:t + 1],
                                            ALU.subtract, ALU.mult).then_inc(ready, 1)

            nc.vector.memset(zrow, 0.0).then_inc(zero_ready, 1)
            dve.wait_ge(in_x, 16)
            variances(stats(0, T))
            dve.wait_ge(tr_w, 1)
            nc.vector.tensor_copy(wqkT[:, :, :], bank[0][:, 0:2 * C].rearrange("p (a n) -> p a n", a=2)).then_inc(wT_ready, 1)
            dve.wait_ge(tr_ctx, 1)
            nc.vector.tensor_copy(cfT[:, 0:512], bank[1][:, :]).then_inc(ctxT_v, 1)
            nc.vector.tensor_copy(b1T[:, :], bank[0][:, 2 * C:2 * C + HC * N_EXP]).then_inc(wT_ready, 1)
            for h in range(2):
                if h == 1:
                    low(3)
                dve.wait_ge(k_done, h + 1)
                nc.vector.tensor_scalar(kT[:, 512 * h:512 * h + 512], bank[5 + h][:, :], bqk[:, 1:2], None,
                                        ALU.add).then_inc(k_ready, 1)
            normalise(1, ln_ready)
            e_bank = [1, 2, 0, 7]

            def maxima(b):
                dve.wait_ge(energy, b + 1)
                nc.vector.tensor_reduce(out=nmax[:, 2 * b:2 * b + 2],
                                        in_=bank[e_bank[b]][:, :].rearrange("p (j n) -> p j n", j=2),
                                        axis=X, op=ALU.max, negate=True).then_inc(max_ready, 1)

            def probs(b):
                dve.wait_ge(exp_ready, 2 * b + 2)
                step(nc.vector.reciprocal(rinv[:, 2 * b:2 * b + 2], rsum[:, 2 * b:2 * b + 2]))
                for j in range(2):
                    last = nc.vector.tensor_scalar(prob[:, b % 2, j, :], prob[:, b % 2, j, :],
                                                   rinv[:, 2 * b + j:2 * b + j + 1], None, ALU.mult)
                last.then_inc(prob_ready, 1)

            def lnT_copy(b):
                dve.wait_ge(tr_ln, b + 1)
                if b >= 2:
                    dve.wait_ge(mixed, b - 1)
                nc.vector.tensor_copy(lnT[:, b % 2, :, :], bank[3 + b][:, :].rearrange("p (c n) -> p c n", c=2)
                                      ).then_inc(lnT_ready, 1)

            def residual(b):
                dve.wait_ge(mixed, b + 1)
                if b == 0:
                    dve.wait_ge(tg_ready, 1)
                nc.vector.scalar_tensor_tensor(out=xs[:, 2 * b:2 * b + 2, :],
                                               in0=bank[3 + b][:, :].rearrange("p (j n) -> p j n", j=2),
                                               scalar=tg[:, 0:1], in1=xs[:, 2 * b:2 * b + 2, :],
                                               op0=ALU.mult, op1=ALU.add).then_inc(x2_ready, 1)

            def stats_of(b):
                dve.wait_ge(x2_ready, b + 1)
                return stats(2 * b, 2 * b + 2)

            maxima(0)
            maxima(1)
            dve.wait_ge(zero_sent, 32)
            lnT_copy(0)
            probs(0)
            maxima(2)
            lnT_copy(1)
            probs(1)
            maxima(3)
            residual(0)
            lnT_copy(2)
            probs(2)
            low(7)
            residual(1)
            lnT_copy(3)
            probs(3)
            stats_of(0)
            nc.vector.tensor_copy(ident16[:, :], ident)
            nc.vector.tensor_copy(identb[:, :], ident)
            nc.vector.tensor_copy(upper16[:, :], cst[:, C_UP:C_UP + P])
            nc.vector.tensor_copy(iota16[:, :], cst[:, C_IOTA:C_IOTA + P])
            nc.vector.memset(ones16[:, :], 1.0)
            nc.vector.memset(M16[:, 0:T - 1, :], 0.0)
            nc.vector.tensor_scalar(col0[:, :], cst[:, C_IOTA:C_IOTA + P], 0.0, None,
                                    ALU.is_equal).then_inc(small_ready, 1)
            residual(2)
            stats_of(1)
            low(11)
            residual(3)
            stats_of(2)
            variances(stats_of(3))
            normalise(2, xn_ready)
            for b in range(B):
                dve.wait_ge(xn_ready, 2 * b + 2)
                if b == 0:
                    dve.wait_ge(mixed, B)
                hi_p, lo_p = split[b][:, :, 0:D], split[b][:, :, D:2 * D].bitcast(BF16)
                step(nc.vector.tensor_copy(hi_p, lnx[:, 2 * b:2 * b + 2, :]))
                nc.vector.tensor_tensor(out=lo_p, in0=lnx[:, 2 * b:2 * b + 2, :], in1=hi_p,
                                        op=ALU.subtract).then_inc(split_ready, 1)
                if b == 0:
                    low(15)
            low(19)

            def e_bc(ap):
                return ap.unsqueeze(1).broadcast_to(te)

            def t_bc(ap):
                return ap.unsqueeze(2).broadcast_to(te)

            dve.wait_ge(logits, B)
            lg_ps = bank[1][:, 0:T * N_EXP].rearrange("p (t e) -> p t e", t=T)
            step(nc.vector.tensor_copy(lg[:, :, :], lg_ps))
            for k in range(TOPK):
                src = lg[:, :, :] if k == 0 else lg2
                step(nc.vector.tensor_reduce(out=top[:, k, :], in_=src, axis=X, op=ALU.max))
                step(nc.vector.tensor_tensor(out=sc, in0=src, in1=t_bc(top[:, k, :]), op=ALU.is_equal))
                step(nc.vector.tensor_tensor(out=sc, in0=sc, in1=e_bc(desc), op=ALU.mult))
                step(nc.vector.tensor_reduce(out=pick[:, k, :], in_=sc, axis=X, op=ALU.max))
                step(nc.vector.tensor_tensor(out=E16[:, k, :, :], in0=e_bc(desc), in1=t_bc(pick[:, k, :]), op=ALU.is_equal))
                if k == 0:
                    step(nc.vector.scalar_tensor_tensor(out=lg2, in0=E16[:, 0, :, :], scalar=-BIG,
                                                        in1=lg[:, :, :], op0=ALU.mult, op1=ALU.add))
            nc.vector.tensor_tensor(out=M16[:, T - 1:2 * T - 1, :], in0=E16[:, 0, :, :], in1=E16[:, 1, :, :],
                                    op=ALU.add).then_inc(choice_ready, 1)
            nc.vector.tensor_tensor(out=dlg[:, :, :], in0=lg[:, :, :], in1=t_bc(top[:, 0, :]),
                                    op=ALU.subtract).then_inc(dlg_ready, 1)
            low(23)
            dve.wait_ge(counted, 1)
            step(nc.vector.tensor_reduce(out=tot[:, :, :],
                                         in_=bank[2][:, P:2 * P].rearrange("p (k t e) -> p k e t", k=TOPK, t=T),
                                         axis=X, op=ALU.add))
            step(nc.vector.tensor_tensor(out=nexp[:, :], in0=tot[:, 0, :], in1=tot[:, 1, :], op=ALU.add))
            ee = [P, N_EXP, N_EXP]
            step(nc.vector.tensor_tensor(out=ge[:, :, :], in0=nexp[:, :].unsqueeze(2).broadcast_to(ee),
                                         in1=thr.unsqueeze(1).broadcast_to(ee), op=ALU.is_ge))
            step(nc.vector.tensor_reduce(out=cnt[:, :], in_=ge[:, :, :], axis=X, op=ALU.add))
            step(nc.vector.tensor_scalar(cnt[:, :], cnt[:, :], 1.0, None, ALU.add))
            step(nc.vector.tensor_tensor(out=ge[:, :, :], in0=lt, in1=cnt[:, :].unsqueeze(1).broadcast_to(ee), op=ALU.mult))
            step(nc.vector.tensor_reduce(out=st_[:, :], in_=ge[:, :, :], axis=X, op=ALU.add))
            step(nc.vector.tensor_scalar(sbase[:, :], st_[:, :], float(P), 1.0, ALU.mult, ALU.add))
            step(nc.vector.tensor_tensor(out=slotb, in0=bank[2][:, 0:T * N_EXP].rearrange("p (t e) -> p t e", t=T),
                                         in1=e_bc(sbase[:, :]), op=ALU.add))
            kte = [P, TOPK, T * N_EXP]
            e2 = E16[:, :, :, :].rearrange("p k t e -> p k (t e)")
            sp2 = sprod.rearrange("p k t e -> p k (t e)")
            step(nc.vector.tensor_tensor(out=sp2, in0=e2,
                                         in1=slotb.rearrange("p t e -> p (t e)").unsqueeze(1).broadcast_to(kte),
                                         op=ALU.mult))
            step(nc.vector.tensor_reduce(out=r_f[:, :], in_=sprod.rearrange("p k t e -> p (k t) e"),
                                         axis=X, op=ALU.add))
            step(nc.vector.tensor_copy(slot[:, :], r_f[:, :]))
            nc.vector.tensor_scalar(blk_i[:, :], slot[:, :], 7, None, ALU.logical_shift_right)
            step(nc.vector.tensor_scalar(r_i[:, :], slot[:, :], P - 1, None, ALU.bitwise_and))
            nc.vector.tensor_copy(blk_f[:, :], blk_i[:, :])
            step(nc.vector.tensor_copy(r_f[:, :], r_i[:, :]))
            kb = [P, TOPK * T, BLOCKS]
            step(nc.vector.tensor_tensor(out=ohb[:, :, :], in0=iota_b.unsqueeze(1).broadcast_to(kb),
                                         in1=blk_f[:, :].unsqueeze(2).broadcast_to(kb), op=ALU.is_equal))
            for k in range(TOPK):
                nc.vector.tensor_tensor(out=ohc[:, k * T:(k + 1) * T, :], in0=ohb[:, k * T:(k + 1) * T, :],
                                        in1=tokp1.unsqueeze(2).broadcast_to([P, T, BLOCKS]), op=ALU.mult)
            step(nc.vector.tensor_tensor(out=ge[:, 0, :], in0=st_[:, :], in1=cst[:, C_ID:C_ID + N_EXP], op=ALU.mult))
            step(nc.vector.tensor_reduce(out=scol[:, :], in_=ge[:, 0, :], axis=X, op=ALU.add))
            nc.vector.tensor_scalar(dumb[:, :], iota_b, scol[:, :], dcode, ALU.is_equal, ALU.mult)
            for kt in range(TOPK * T):
                last = nc.vector.tensor_scalar(ohr[:, kt, :], iota16[:, :], r_f[:, kt:kt + 1], None, ALU.is_equal)
                last.then_inc(onehot_ready, 1)
            step(nc.vector.tensor_tensor(out=en[:, :], in0=st_[:, :], in1=cnt[:, :], op=ALU.add))
            be = [P, BLOCKS, N_EXP]
            step(nc.vector.tensor_tensor(out=ebge, in0=iota_b.unsqueeze(2).broadcast_to(be),
                                         in1=en[:, :].unsqueeze(1).broadcast_to(be), op=ALU.is_ge))
            step(nc.vector.tensor_reduce(out=ebf[:, :], in_=ebge, axis=X, op=ALU.add))
            nc.vector.tensor_scalar(eb[:, :], ebf[:, :], float(N_EXP - 1), None, ALU.min)
            dve.wait_ge(codes_done, 1)
            code = bank[0][:, 0:BLOCKS]
            nc.vector.tensor_copy(gidx[:, :], code).then_inc(index_ready, 1)
            step(nc.vector.tensor_scalar(yt1[:, :], code, 0.0, float(SKIP), ALU.is_equal, ALU.mult))
            step(nc.vector.tensor_tensor(out=yt2[:, :], in0=yt1[:, :], in1=code, op=ALU.add))
            nc.vector.scalar_tensor_tensor(out=yidx[:, :], in0=bank[0][:, BLOCKS:2 * BLOCKS], scalar=float(SECOND),
                                           in1=yt2[:, :], op0=ALU.mult, op1=ALU.add).then_inc(index_ready, 1)

            low(27)
            low(31)

            def xT_copy(j, u):
                i = 2 * j + u
                dve.wait_ge(tr_x, i + 1)
                if not isinstance(j, int) or j:
                    dve.wait_ge(h_done, 2 * i - 2)
                nc.vector.tensor_copy(xT[:, u, :].bitcast(I32),
                                      bank[2 + u][:, 0:D].bitcast(I32)).then_inc(xT_ready, 1)

            def hidden_split(j, u, half):
                i = 2 * j + u
                if half == 0 and (not isinstance(j, int) or j):
                    dve.wait_ge(y_done, i - 1)
                dve.wait_ge(gelu_done, 2 * i + half + 1)
                hs = hidden[u][:, 512 * half:512 * half + 512].rearrange("p (c n) -> p c n", n=P)
                hh, hl = h_hi[:, u, 4 * half:4 * half + 4, :], h_lo[:, u, 4 * half:4 * half + 4, :]
                nc.vector.tensor_copy(hh, hs).then_inc(h_ready, 1)
                dve.wait_ge(h_ready, 4 * i + 2 * half + 1)
                nc.vector.tensor_tensor(out=hl, in0=hs, in1=hh, op=ALU.subtract).then_inc(h_ready, 1)

            def y_copy(j, u):
                i = 2 * j + u
                dve.wait_ge(y_done, i + 1)
                if not isinstance(j, int) or j:
                    dve.wait_ge(scattered[u], 16 * j)
                nc.vector.tensor_copy(ysb[:, u, :], bank[4 + u][:, 0:D]).then_inc(y_ready, 1)

            def fetch_w1(i, u):
                e = dve.value_load(eb[0:1, bass.ds(i, 1)], min_val=0, max_val=N_EXP - 1)
                if not isinstance(i, int) or i > 3:
                    dve.wait_ge(h_done, 2 * i - 2)
                for h in range(2):
                    nc.vector.tensor_copy(w1f[:, u, h, :].bitcast(I32).unsqueeze(1),
                                          w1_words[h][:, bass.ds(e, 1), 0:QW]).then_inc(w1_fetched, 1)

            xT_copy(0, 0)
            xT_copy(0, 1)
            dve.wait_ge(elg_ready, 1)
            step(nc.vector.tensor_reduce(out=z[:, :], in_=elg[:, :, :], axis=X, op=ALU.add))
            step(nc.vector.reciprocal(z[:, :], z[:, :]))
            step(nc.vector.tensor_tensor(out=sp2, in0=e2,
                                         in1=elg[:, :, :].rearrange("p t e -> p (t e)").unsqueeze(1).broadcast_to(kte),
                                         op=ALU.mult))
            step(nc.vector.tensor_reduce(out=wk[:, :, :], in_=sprod, axis=X, op=ALU.add))
            step(nc.vector.scalar_tensor_tensor(out=wk[:, :, :], in0=wk[:, :, :], scalar=tg[:, 1:2],
                                                in1=z[:, :].unsqueeze(1).broadcast_to([P, TOPK, T]),
                                                op0=ALU.mult, op1=ALU.mult))
            step(nc.vector.tensor_scalar(act_f[:, :, :], tot[:, :, :], 0.0, None, ALU.is_gt))
            for k in range(TOPK):
                step(nc.vector.tensor_tensor(out=dcat[:, k, :, :], in0=e_bc(act_f[:, k, :]), in1=E16[:, k, :, :],
                                             op=ALU.subtract))
                step(nc.vector.tensor_tensor(out=dcat[:, k, :, :], in0=dcat[:, k, :, :], in1=t_bc(wk[:, k, :]),
                                             op=ALU.mult))
                step(nc.vector.tensor_tensor(out=sprod[:, k, :, :], in0=e_bc(act_f[:, k, :]), in1=t_bc(wk[:, k, :]),
                                             op=ALU.mult))
            nc.vector.tensor_tensor(out=cat[:, :, 0:N_EXP], in0=dcat[:, 0, :, :], in1=dcat[:, 1, :, :], op=ALU.add)
            step(nc.vector.tensor_tensor(out=cat[:, :, N_EXP:2 * N_EXP], in0=sprod[:, 0, :, :], in1=sprod[:, 1, :, :],
                                         op=ALU.add))
            hidden_split(0, 0, 0)
            xT_copy(1, 0)
            hidden_split(0, 0, 1)
            dve.wait_ge(*low_done(QUARTERS - 2))
            dve.wait_ge(lo_dve, N_EXP)
            fetch_w1(2, 0)
            hidden_split(0, 1, 0)
            y_copy(0, 0)

            def pair(j, last=False):
                xT_copy(j, 1)
                hidden_split(j - 1, 1, 1)
                fetch_w1(2 * j + 1, 1)
                hidden_split(j, 0, 0)
                y_copy(j - 1, 1)
                if not last:
                    xT_copy(j + 1, 0)
                hidden_split(j, 0, 1)
                if not last:
                    fetch_w1(2 * j + 2, 0)
                hidden_split(j, 1, 0)
                y_copy(j, 0)

            with dve.Fori(1, JN - 1) as j:
                pair(j)
            pair(JN - 1, last=True)
            hidden_split(JN - 1, 1, 1)
            y_copy(JN - 1, 1)

            dve.wait_ge(tr_cat, 1)
            for half in range(2):
                nc.vector.tensor_copy(catT[:, 512 * half:512 * half + 512],
                                      bank[half][0:2 * N_EXP, :]).then_inc(catT_ready, 1)
            for q in range(T // 2):
                dve.wait_ge(in_y[q], 32)
                dve.wait_ge(const_done, q + 1)
                for t in (2 * q, 2 * q + 1):
                    last = nc.vector.scalar_tensor_tensor(
                        out=y_in[:, t, :], in0=y_in[:, t, :], scalar=wk[:, 0, t:t + 1],
                        in1=bank[(2, 3, 6, 7)[q]][:, (t % 2) * D:(t % 2 + 1) * D], op0=ALU.mult, op1=ALU.add)
                step(last)
                for t in (2 * q, 2 * q + 1):
                    nc.vector.scalar_tensor_tensor(
                        out=y_in[:, t, :], in0=y_in[:, T + t, :], scalar=wk[:, 1, t:t + 1],
                        in1=y_in[:, t, :], op0=ALU.mult, op1=ALU.add).then_inc(out_ready, 1)

        @block.tensor
        def _(pe):
            mm, tr = nc.tensor.matmul, nc.tensor.transpose
            e_bank = [1, 2, 0, 7]
            pe.wait_ge(in_cst, 16)
            pe.wait_ge(in_wqk, 64)
            pe.wait_ge(in_bias, 32)
            for a in range(2):
                tr(bank[0][:, C * a:C * a + C], wqk[:, a, :], ident)
            tr(bank[0][:, 2 * C:2 * C + HC * N_EXP], b1r, cst[0:HC * N_EXP, C_ID:C_ID + HC * N_EXP]).then_inc(tr_w, 1)
            pe.wait_ge(in_ctx, 16)
            for h in range(2):
                for t in range(4):
                    last = tr(bank[1 + h][:, P * t:P * t + P], cf[:, 4 * h + t, :], ident)
                last.then_inc(tr_ctx, 1)
            pe.wait_ge(wT_ready, 1)
            for h in range(2):
                if h == 0:
                    pe.wait_ge(ctxT_v, 1)
                else:
                    pe.wait_ge(ctxT_a, 1)
                mm(bank[3 + h][:, :], wqkT[:, 0, :], cfT[:, 512 * h:512 * h + 512], start=True, stop=True).then_inc(q_done, 1)
                mm(bank[5 + h][:, :], wqkT[:, 1, :], cfT[:, 512 * h:512 * h + 512], start=True, stop=True).then_inc(k_done, 1)

            def energies(b):
                pe.wait_ge(q_ready, b // 2 + 1)
                pe.wait_ge(k_ready, b // 2 + 1)
                if b == 2:
                    pe.wait_ge(wT_ready, 2)
                for j in range(2):
                    last = mm(bank[e_bank[b]][:, L * j:L * j + L], qT[:, L * b + P * j:L * b + P * j + P],
                              kT[:, L * b:L * b + L], start=True, stop=True)
                last.then_inc(energy, 1)

            def lnT_tr(b):
                pe.wait_ge(ln_ready, 2 * b + 2)
                pe.wait_ge(q_ready, 2)
                pe.wait_ge(k_ready, 2)
                for c in range(2):
                    for j in range(2):
                        last = tr(bank[3 + b][:, L * c + P * j:L * c + P * j + P], lnx[:, 2 * b + j, P * c:P * c + P], ident)
                last.then_inc(tr_ln, 1)

            def probT_tr(b):
                pe.wait_ge(prob_ready, b + 1)
                for c in range(2):
                    for j in range(2):
                        last = tr(bank[e_bank[b]][:, L * c + P * j:L * c + P * j + P], prob[:, b % 2, j, P * c:P * c + P], ident)
                last.then_inc(tr_p, 1)

            def mix(b):
                pe.wait_ge(lnT_ready, b + 1)
                pe.wait_ge(probT_ready, b + 1)
                for j in range(2):
                    for c in range(2):
                        last = mm(bank[3 + b][:, L * j:L * j + L], lnT[:, b % 2, c, P * j:P * j + P],
                                  probT[:, b % 2, c, :], start=(c == 0), stop=(c == 1))
                last.then_inc(mixed, 1)

            for b in range(B):
                energies(b)
            lnT_tr(0)
            lnT_tr(1)
            probT_tr(0)
            lnT_tr(2)
            mix(0)
            probT_tr(1)
            lnT_tr(3)
            mix(1)
            probT_tr(2)
            mix(2)
            probT_tr(3)
            mix(3)
            pe.wait_ge(in_router, 32)

            def xnT_tr(b):
                pe.wait_ge(xn_ready, 2 * b + 2)
                for c in range(2):
                    for j in range(2):
                        last = tr(bank[e_bank[b]][:, L * c + P * j:L * c + P * j + P], lnx[:, 2 * b + j, P * c:P * c + P], ident)
                last.then_inc(tr_xn, 1)

            def router_hidden(b):
                pe.wait_ge(xnT_ready, b + 1)
                pe.wait_ge(x2_ready, b + 1)
                for c in range(DC):
                    last = mm(bank[3 + b][:, 0:L], rw1_s[:, c, :], xnT[:, b % 2, c, :], start=(c == 0), stop=(c == DC - 1))
                last.then_inc(rh_done, 1)

            def router_logits(b):
                pe.wait_ge(rh_ready, b + 1)
                for j in range(2):
                    t = 2 * b + j
                    last = mm(bank[1][:, t * N_EXP:(t + 1) * N_EXP], rh[:, b % 2, P * j:P * j + P], rw2_s[:, :],
                              start=True, stop=True)
                last.then_inc(logits, 1)

            xnT_tr(0)
            xnT_tr(1)
            router_hidden(0)
            xnT_tr(2)
            router_hidden(1)
            router_logits(0)
            xnT_tr(3)
            router_hidden(2)
            router_logits(1)
            router_hidden(3)
            router_logits(2)
            router_logits(3)

            pe.wait_ge(small_ready, 1)
            pe.wait_ge(choice_ready, 1)
            n = T * N_EXP
            m2 = M16[:, :, :].rearrange("p t e -> p (t e)")
            mm(bank[2][:, P:2 * P], ones16[:, :], E16[:, :, :, :].rearrange("p k t e -> p (k t e)"), start=True, stop=True)
            mm(bank[2][:, 0:n], upper16[:, :], m2[:, (T - 1) * N_EXP:(2 * T - 1) * N_EXP], start=True, stop=False)
            for s in range(1, T):
                last = mm(bank[2][:, 0:n], ones16[:, :], m2[:, (T - 1 - s) * N_EXP:(2 * T - 1 - s) * N_EXP],
                          start=False, stop=(s == T - 1))
            last.then_inc(counted, 1)
            pe.wait_ge(onehot_ready, 1)
            mm(bank[0][:, 0:BLOCKS], col0[:, :], dumb[:, :], start=True, stop=False)
            for kt in range(TOPK * T):
                pe.wait_ge(onehot_ready, kt + 1)
                mm(bank[0][:, 0:BLOCKS], ohr[:, kt, :], ohc[:, kt, :], start=False, stop=(kt == TOPK * T - 1))
            for kt in range(T, TOPK * T):
                last = mm(bank[0][:, BLOCKS:2 * BLOCKS], ohr[:, kt, :], ohb[:, kt, :], start=(kt == T),
                          stop=(kt == TOPK * T - 1))
            last.then_inc(codes_done, 1)
            pe.wait_ge(index_ready, 1)

            def tokens_tr(j, u):
                pe.wait_ge(gathered[u], 16 * (j + 1))
                for c in range(2 * DC):
                    if c < DC:
                        last = tr(bank[2 + u][:, :].bitcast(F16)[:, P * c:P * c + P], xg[:, u, P * c:P * c + P], ident16[:, :])
                    else:
                        last = tr(bank[2 + u][:, :].bitcast(BF16)[:, P * c:P * c + P],
                                  xg[:, u, P * c:P * c + P].bitcast(BF16), identb[:, :])
                last.then_inc(tr_x, 1)

            def expert_of(i):
                return pe.value_load(eb[0:1, bass.ds(i, 1)], min_val=0, max_val=N_EXP - 1)

            experts = [pe.alloc_register(f"expert_{n}") for n in ("before", "even")]

            def load_experts(j):
                for k, r in enumerate(experts):
                    pe.load(r, eb[0:1, bass.ds(2 * j - 1 + k, 1)])

            def up(i, u, e, c):
                if c == 0:
                    pe.wait_ge(xT_ready, i + 1)
                    if e is None:
                        pe.wait_ge(w1_fetched, 2 * i - 2)
                xh = xT[:, u, 0:D].rearrange("p (d n) -> p d n", d=DC)
                xl = xT[:, u, D:2 * D].bitcast(BF16).rearrange("p (d n) -> p d n", d=DC)
                o = bank[(0 if u == 0 else 6) + c // 4][:, (c % 4) * P:(c % 4 + 1) * P]
                cs = slice(c * P, (c + 1) * P)
                for d in range(DC):
                    if e is None:
                        wh, wl = w1f_hi[u][:, d, cs], w1f_lo[u][:, d, cs]
                    else:
                        wh, wl = w1_hi[:, bass.ds(e, 1), d, cs], w1_lo[:, bass.ds(e, 1), d, cs]
                    mm(o, wh, xh[:, d, :], start=(d == 0), stop=False)
                    mm(o, wh, xl[:, d, :], start=False, stop=False)
                    last = mm(o, wl, xh[:, d, :], start=False, stop=(d == DC - 1))
                if c % 4 == 3:
                    last.then_inc(h_done, 1)

            def down(i, u, e, c):
                if c % 4 == 0:
                    pe.wait_ge(h_ready, 4 * i + c // 2 + 2)
                o = bank[4 + u][:, 0:D]
                mm(o, h_hi[:, u, c, :], w2_hi[:, bass.ds(e, 1), 1, c, :], start=(c == 0), stop=False)
                mm(o, h_hi[:, u, c, :], w2_lo[:, bass.ds(e, 1), 1, c, :], start=False, stop=False)
                last = mm(o, h_lo[:, u, c, :], w2_hi[:, bass.ds(e, 1), 1, c, :], start=False, stop=(c == HC - 1))
                if c == HC - 1:
                    last.then_inc(y_done, 1)

            tokens_tr(0, 0)
            pe.wait_ge(*low_done(QPE - 1))
            pe.wait_ge(*low_done(QPE - 2))
            tokens_tr(0, 1)
            e0 = expert_of(0)
            for c in range(HC):
                up(0, 0, e0, c)
            pe.wait_ge(*low_done(2 * QPE - 1))
            pe.wait_ge(*low_done(2 * QPE - 2))
            tokens_tr(1, 0)
            e1 = expert_of(1)
            for c in range(HC):
                up(1, 1, e1, c)
                down(0, 0, e0, c)
            pe.wait_ge(*low_done(QUARTERS - 1))
            pe.wait_ge(*low_done(QUARTERS - 2))

            def pair(j, last=False):
                i = 2 * j
                ea, eb_ = [pe.snap(r, min_val=0, max_val=N_EXP - 1) for r in experts]
                tokens_tr(j, 1)
                for c in range(HC):
                    up(i, 0, None, c)
                    down(i - 1, 1, ea, c)
                if not last:
                    load_experts(j + 1)
                    tokens_tr(j + 1, 0)
                for c in range(HC):
                    up(i + 1, 1, None, c)
                    down(i, 0, eb_, c)

            load_experts(1)
            with pe.Fori(1, JN - 1) as j:
                pair(j)
            pair(JN - 1, last=True)
            el = expert_of(BLOCKS - 1)

            def residual_to(q):
                mm(bank[(2, 3, 6, 7)[q]][:, :], ident, xs[:, 2 * q:2 * q + 2, :].rearrange("p t n -> p (t n)"),
                   start=True, stop=False)

            residual_to(0)
            for c in range(HC):
                down(BLOCKS - 1, 1, el, c)

            pe.wait_ge(gelu_done, 2 * BLOCKS)
            pe.wait_ge(xT_ready, BLOCKS)
            for t in range(T):
                last = tr(bank[t // 4][0:2 * N_EXP, P * (t % 4):P * (t % 4) + P], cat[:, t, :], ident)
            last.then_inc(tr_cat, 1)
            for q in range(1, T // 2):
                residual_to(q)
            pe.wait_ge(catT_ready, 2)
            pe.wait_ge(in_cb, 16)
            for t in range(T):
                last = mm(bank[(2, 3, 6, 7)[t // 2]][:, (t % 2) * D:(t % 2 + 1) * D], catT[:, P * t:P * t + P],
                          cb[:, :], start=False, stop=(t % 2 == 1))
                if t % 2:
                    last.then_inc(const_done, 1)


_INS = ['x', 'ctx_1024', 'g_xattn', 'g_ffn', 'L0_xattn_Wq', 'L0_xattn_bq', 'L0_xattn_Wk', 'L0_xattn_bk',
        'L0_ffn_rw1', 'L0_ffn_rw2', 'L0_ffn_w1', 'L0_ffn_b1', 'L0_ffn_w2', 'L0_ffn_b2']


def shape_constants():
    import numpy as np
    c = np.zeros((P, C_ALL), np.float32)
    p = np.arange(P)
    c[:, C_ID:C_ID + P] = np.eye(P)
    c[:, C_UP:C_UP + P] = p[:, None] < p[None, :]
    c[:, C_IOTA:C_IOTA + P] = p[None, :]
    c[:, C_DESC:C_DESC + N_EXP] = N_EXP - np.arange(N_EXP)
    e = np.arange(N_EXP)
    c[:, C_LT:C_LT + N_EXP * N_EXP] = (e[None, :] < e[:, None]).reshape(-1)
    c[:, C_THR:C_THR + N_EXP] = P * (1 + e)
    c[:, C_BLK:C_BLK + BLOCKS] = np.arange(BLOCKS)
    c[:, C_TOK:C_TOK + T] = 1 + p[:, None] + P * np.arange(T)[None, :]
    c[:N_EXP, C_DUM] = ZERO_TOKEN + e
    return c


def kernel(**inputs):
    import numpy as _np
    import concourse.bacc as _bacc
    from concourse import mybir as _mybir
    from concourse.bass_utils import run_bass_kernel_spmd as _run

    nc = _bacc.Bacc("TRN2", target_bir_lowering=False, num_devices=1)
    arrays, args = {}, []
    for name in _INS:
        a = _np.ascontiguousarray(inputs[name])
        arrays[f"in_{name}"] = a
        args.append(nc.dram_tensor(f"in_{name}", a.shape, _mybir.dt.from_np(a.dtype), kind="ExternalInput").ap())
    a = shape_constants()
    arrays["in_consts"] = a
    args.append(nc.dram_tensor("in_consts", a.shape, _mybir.dt.from_np(a.dtype), kind="ExternalInput").ap())
    args.append(nc.dram_tensor("out_0", (B, L, D), _mybir.dt.float32, kind="ExternalOutput").ap())
    flamingo_moe_kernel(nc, *args)
    r = _run(nc, [arrays], core_ids=[0])
    return r.results[0]["out_0"]
```

```python
import concourse.bass as bass
from concourse import mybir
from contextlib import ExitStack

P = 128
B, L, D = 4, 256, 256
C = 128
TOK = B * L
T = TOK // P
N_EXP, HID, TOPK = 8, 1024, 2
DC = D // P
HC = HID // P
RH = 128
EPS = 1e-5
BLOCKS = (TOPK * TOK + N_EXP + N_EXP * (P - 1)) // P
SLOTS = 1 << (BLOCKS * P - 1).bit_length()
ROWS_X = 1 + TOK + N_EXP
ZERO_TOKEN = 1 + TOK
SECOND = 2 * TOK
ROWS_Y = SECOND + TOK + 1
SKIP = 8 * TOK
QPE = 4
QUARTERS = QPE * N_EXP
QW = D * HID // P // 2
RING = 6
BIG = 1e30

C_ID, C_UP, C_IOTA = 0, P, 2 * P
C_DESC = 3 * P
C_LT = C_DESC + N_EXP
C_THR = C_LT + N_EXP * N_EXP
C_BLK = C_THR + N_EXP + 1
C_TOK = C_BLK + BLOCKS
C_DUM = C_TOK + T
C_ALL = C_DUM + 1


def flamingo_moe_kernel(nc, x, ctx_in, g_x, g_f, Wq, bq, Wk, bk, rw1, rw2, w1, b1, w2, b2, consts, out):
    F32, F16, BF16, I32 = mybir.dt.float32, mybir.dt.float16, mybir.dt.bfloat16, mybir.dt.int32
    ALU = mybir.AluOpType
    ACT = mybir.ActivationFunctionType
    X = mybir.AxisListType.X

    ctx = ExitStack()
    with ctx:
        def sb(name, shape, dt):
            return ctx.enter_context(nc.sbuf_tensor(name, shape, dt))

        def sem(name):
            return ctx.enter_context(nc.semaphore(name))

        x_table = nc.dram_tensor("x_table", [ROWS_X, 2 * D], F16, kind="Internal").ap()
        y_table = nc.dram_tensor("y_table", [ROWS_Y, D], F32, kind="Internal").ap()

        w_hi = sb("w_hi", [P, QUARTERS, QW], F16)
        w_lo = sb("w_lo", [P, QUARTERS, QW], BF16)
        filler = w_hi[:, QUARTERS - 1, 0:512]
        w1_hi, w1_lo = [w[:, :, :].rearrange("p (e q) n -> p e q n", q=QPE) for w in (w_hi, w_lo)]
        w2_hi, w2_lo = [w[:, :, :].rearrange("p (e j q) (c n) -> p e j (q c) n", j=2, q=2, n=D) for w in (w_hi, w_lo)]
        stage = sb("stage", [P, RING, QW], F32)
        w1_words = [w[:, :, :].bitcast(mybir.dt.int32).rearrange("p (e q) n -> p e (q n)", q=QPE) for w in (w_hi, w_lo)]
        FETCH_SLOT = QUARTERS % RING
        w1f = stage[:, FETCH_SLOT:FETCH_SLOT + 4, :].rearrange("p (u h) n -> p u h n", u=2)
        w1f_hi = [w1f[:, u, 0, :].bitcast(F16).rearrange("p (d n) -> p d n", d=DC) for u in range(2)]
        w1f_lo = [w1f[:, u, 1, :].bitcast(BF16).rearrange("p (d n) -> p d n", d=DC) for u in range(2)]
        y_in = stage[:, :, :].rearrange("p a (b n) -> p (a b) n", n=D)

        cst = sb("cst", [P, C_ALL], F32)
        xs = sb("xs", [P, T, D], F32)
        lnx = sb("lnx", [P, T, D], F32)
        cf = sb("cf", [P, T, C], F32)
        cfT = sb("cfT", [P, TOK], F32)
        qT = sb("qT", [P, TOK], F32)
        kT = sb("kT", [P, TOK], F32)
        prob = sb("prob", [P, 2, 2, L], F32)
        probT = sb("probT", [P, 2, 2, L], F32)
        lnT = sb("lnT", [P, 2, 2, L], F32)
        split = [v[:, :].bitcast(F16).rearrange("p (u j n) -> p u j n", u=2, j=2)[:, u]
                 for v in (cfT, probT[:, :, :, :].rearrange("p a b n -> p (a b n)")) for u in range(2)]
        xnT = kT[:, :].rearrange("p (u c n) -> p u c n", u=2, c=2)
        rh = qT[:, 0:2 * L].rearrange("p (u n) -> p u n", u=2)
        early = prob[:, :, :, :].rearrange("p a b n -> p (a b n)")
        wqk = early[:, 0:2 * C].rearrange("p (a n) -> p a n", a=2)
        wqkT = early[:, 2 * C:4 * C].rearrange("p (a n) -> p a n", a=2)
        b1r = early[0:HC * N_EXP, 4 * C:4 * C + P]
        rw1_s = sb("rw1_s", [P, DC, RH], F32)
        rw2_s = sb("rw2_s", [P, N_EXP], F32)
        b1T = sb("b1T", [P, HC * N_EXP], F32)
        cb = sb("cb", [2 * N_EXP, D], F32)
        bqk = sb("bqk", [P, 2], F32)
        gate = sb("gate", [P, 2], F32)
        tg = sb("tg", [P, 2], F32)
        bns = sb("bns", [P, T, 6], F32)
        mv = sb("mv", [P, T, 2], F32)
        rstd = sb("rstd", [P, T], F32)
        nmax = sb("nmax", [P, T], F32)
        rsum = sb("rsum", [P, T], F32)
        rinv = sb("rinv", [P, T], F32)
        ident16 = sb("ident16", [P, P], F16)
        identb = sb("identb", [P, P], BF16)
        upper16 = sb("upper16", [P, P], F16)
        ones16 = sb("ones16", [P, P], F16)
        iota16 = sb("iota16", [P, P], F16)
        col0 = sb("col0", [P, P], F16)
        te = [P, T, N_EXP]
        tmp = cf[:, :, :].rearrange("p t n -> p (t n)")
        TE = T * N_EXP
        lg2 = tmp[:, 0:TE].rearrange("p (t e) -> p t e", t=T)
        sc = tmp[:, TE:2 * TE].rearrange("p (t e) -> p t e", t=T)
        slotb = tmp[:, 2 * TE:3 * TE].rearrange("p (t e) -> p t e", t=T)
        sprod = qT[:, 2 * L - 4 * TE:2 * L - 2 * TE].rearrange("p (k t e) -> p k t e", k=TOPK, t=T)
        dcat = qT[:, 2 * L - 2 * TE:2 * L].rearrange("p (k t e) -> p k t e", k=TOPK, t=T)
        ebge = tmp[:, 7 * TE:7 * TE + BLOCKS * N_EXP].rearrange("p (b e) -> p b e", b=BLOCKS)
        dlg = sb("dlg", te, F32)
        elg = sb("elg", te, F32)
        top = sb("top", [P, TOPK, T], F32)
        pick = sb("pick", [P, TOPK, T], F32)
        E16 = sb("E16", [P, TOPK, T, N_EXP], F16)
        M16 = sb("M16", [P, 2 * T - 1, N_EXP], F16)
        tot = sb("tot", [P, TOPK, N_EXP], F32)
        nexp = sb("nexp", [P, N_EXP], F32)
        ge = sb("ge", [P, N_EXP, N_EXP + 1], F32)
        ltc = sb("ltc", [P, N_EXP, N_EXP], F32)
        cnt = sb("cnt", [P, N_EXP], F32)
        st_ = sb("st_", [P, N_EXP], F32)
        en = sb("en", [P, N_EXP], F32)
        slot_f = sb("slot_f", [P, TOPK * T], F32)
        slot = sb("slot", [P, TOPK * T], I32)
        blk_i = sb("blk_i", [P, TOPK * T], I32)
        r_i = sb("r_i", [P, TOPK * T], I32)
        blk_f = sb("blk_f", [P, TOPK * T], F32)
        r_f = sb("r_f", [P, TOPK * T], F32)
        scol = sb("scol", [P, 1], F32)
        dumb = sb("dumb", [P, BLOCKS], F16)
        oh = lnT[:, :, :, :].rearrange("p a b n -> p (a b n)").bitcast(F16)
        ohb = oh[:, 0:TOPK * T * BLOCKS].rearrange("p (k n) -> p k n", n=BLOCKS)
        ohr = prob[:, :, :, :].rearrange("p a b n -> p (a b n)").bitcast(F16).rearrange(
            "p (k n) -> p k n", n=P)
        ebf = sb("ebf", [P, BLOCKS], F32)
        eb = sb("eb", [P, BLOCKS], I32)
        used_f = sb("used_f", [P, 3], F32)
        used_i = sb("used_i", [P, 3], I32)
        gidx = sb("gidx", [P, BLOCKS], I32)
        yidx = sb("yidx", [P, BLOCKS], I32)
        yt1 = sb("yt1", [P, BLOCKS], F32)
        yt2 = sb("yt2", [P, BLOCKS], F32)
        gcol = sb("gcol", [P, 4], I32)
        ycol = sb("ycol", [P, 2], I32)
        held = sb("held", [P, 1], F32)
        warm = sb("warm", [P, 1], F32)
        z = sb("z", [P, T], F32)
        wk = sb("wk", [P, TOPK, T], F32)
        act_f = sb("act_f", [P, TOPK, N_EXP], F32)
        cat = sb("cat", [P, T, 2 * N_EXP], F32)
        catT = kT[0:2 * N_EXP, :]
        xg = probT[:, :, :, :].rearrange("p a b n -> p (a b n)").bitcast(F16).rearrange(
            "p (u n) -> p u n", u=4)
        xT = cfT[:, 0:2 * D].bitcast(F16).rearrange("p (u n) -> p u n", u=2)
        lnx_flat = lnx[:, :, :].rearrange("p t n -> p (t n)")
        hidden = [lnx_flat[:, 0:HID], lnx_flat[:, HID:2 * HID]]
        h_hi = cf[:, :, :].rearrange("p t n -> p (t n)").bitcast(F16).rearrange(
            "p (u c n) -> p u c n", u=2, c=HC)
        h_lo = lnT[:, :, :, :].rearrange("p a b n -> p (a b n)").bitcast(BF16).rearrange(
            "p (u c n) -> p u c n", u=2, c=HC)
        ysb = qT[:, 2 * L:4 * L].rearrange("p (u n) -> p u n", u=2)
        zrow = lnT[0:N_EXP, 0, 0, :].bitcast(F16)

        bank = [ctx.enter_context(nc.psum_tensor(f"bank{i}", [P, 512], F32)) for i in range(8)]

        ident = cst[:, C_ID:C_ID + P]
        desc = cst[:, C_DESC:C_DESC + N_EXP]
        lt = cst[:, C_LT:C_LT + N_EXP * N_EXP].rearrange("p (a b) -> p a b", a=N_EXP)
        thr = cst[:, C_THR:C_THR + N_EXP + 1]
        iota_b = cst[:, C_BLK:C_BLK + BLOCKS]
        tokp1 = cst[:, C_TOK:C_TOK + T]
        dcode = cst[:, C_DUM:C_DUM + 1]

        in_cst, in_ctx, in_wqk, in_x, in_gate = [sem(n) for n in ("in_cst", "in_ctx", "in_wqk", "in_x", "in_gate")]
        in_router, in_bias = sem("in_router"), sem("in_bias")
        in_w = [sem(f"in_w{r}") for r in range(RING)]
        hi_ready, lo_pool, lo_dve = sem("hi_ready"), sem("lo_pool"), sem("lo_dve")
        v_step = sem("v_step")
        small_ready, zero_ready, zero_sent = sem("small_ready"), sem("zero_ready"), sem("zero_sent")
        var_ready, std_ready, ln_ready = sem("var_ready"), sem("std_ready"), sem("ln_ready")
        tg_ready = sem("tg_ready")
        tr_w, tr_ctx = sem("tr_w"), sem("tr_ctx")
        wT_ready, ctxT_a, ctxT_v = sem("wT_ready"), sem("ctxT_a"), sem("ctxT_v")
        q_done, k_done, q_ready, k_ready = sem("q_done"), sem("k_done"), sem("q_ready"), sem("k_ready")
        energy, max_ready, exp_ready, prob_ready = sem("energy"), sem("max_ready"), sem("exp_ready"), sem("prob_ready")
        tr_ln, lnT_ready, tr_p, probT_ready = sem("tr_ln"), sem("lnT_ready"), sem("tr_p"), sem("probT_ready")
        mixed, x2_ready, xn_ready = sem("mixed"), sem("x2_ready"), sem("xn_ready")
        tr_xn, xnT_ready, rh_done, rh_ready, logits = sem("tr_xn"), sem("xnT_ready"), sem("rh_done"), sem("rh_ready"), sem("logits")
        split_ready, table_sent = sem("split_ready"), [sem("table_sent0"), sem("table_sent1")]
        choice_ready, counted, onehot_ready, codes_done, index_ready = [
            sem(n) for n in ("choice_ready", "counted", "onehot_ready", "codes_done", "index_ready")]
        dlg_ready, elg_ready = sem("dlg_ready"), sem("elg_ready")
        w1_fetched = sem("w1_fetched")
        gcol_ready, ycol_ready = sem("gcol_ready"), sem("ycol_ready")
        gathered = [sem(f"gathered{s}") for s in range(4)]
        used_ready = sem("used_ready")
        scattered = [sem("scattered0"), sem("scattered1")]
        tr_x, xT_ready, h_done, gelu_done, h_ready, y_done, y_ready = [
            sem(n) for n in ("tr_x", "xT_ready", "h_done", "gelu_done", "h_ready", "y_done", "y_ready")]
        tr_cat, catT_ready, in_cb, const_done, out_ready, out_sent = [
            sem(n) for n in ("tr_cat", "catT_ready", "in_cb", "const_done", "out_ready", "out_sent")]
        in_y = [[sem(f"in_y{k}_{q}") for q in range(T // 2)] for k in range(TOPK)]

        DVE_QUARTERS = (3, 7, 11, 15, 18, 25, 27, 28, 30)
        LATE = 25

        def by_dve(q):
            return q in DVE_QUARTERS

        def low_done(q):
            mine = [k for k in range(q + 1) if by_dve(k) == by_dve(q)]
            return (lo_dve if by_dve(q) else lo_pool), len(mine)

        def wait_weights(engine, q):
            for dve in (False, True):
                engine.wait_ge(*low_done(max(k for k in range(q + 1) if by_dve(k) == dve)))

        JN = BLOCKS // 2
        LEAST = (TOPK * TOK + N_EXP + P - 1) // P
        LEAST_LAST, LEAST_ODD = (LEAST - 1) // 2, LEAST // 2

        def count(engine, col, least, most):
            return engine.value_load(used_i[0:1, col:col + 1], min_val=0, max_val=most - least) + least

        def last_pair(engine):
            return count(engine, 0, LEAST_LAST, JN - 1)

        def odd_blocks(engine):
            return count(engine, 1, LEAST_ODD, JN)

        def used_blocks(engine):
            return count(engine, 2, LEAST, BLOCKS)

        def second(j):
            return isinstance(j, int) and j == 1

        def xg_slot(j, u):
            return 2 + u if second(j) else u

        def tokens_in(j, u):
            if second(j):
                return gathered[2 + u], 16
            return gathered[u], 16 if isinstance(j, int) and j == 0 else 16 * j

        block = ctx.enter_context(nc.Block())

        @block.sync
        def _(sp):
            sp.dma_start(cst[:, :], consts).then_inc(in_cst, 16)
            sp.dma_start(cf[:, :, :], ctx_in.rearrange("b (j p) c -> p (b j) c", p=P)).then_inc(in_ctx, 16)
            sp.dma_start(b1r, b1.rearrange("e (c p) -> (e c) p", p=P)).then_inc(in_bias, 16)
            sp.dma_start(cb[N_EXP:2 * N_EXP, :], b2).then_inc(in_bias, 16)
            sp.dma_start(xs[:, :, :], x.rearrange("b (j p) n -> p (b j) n", p=P)).then_inc(in_x, 16)
            sp.dma_start(rw1_s[:, :, :], rw1.rearrange("(d p) n -> p d n", p=P)).then_inc(in_router, 16)
            sp.dma_start(rw2_s[:, :], rw2).then_inc(in_router, 16)

            for q in range(QUARTERS):
                if q >= RING:
                    sp.wait_ge(hi_ready, q - RING + 1)
                    sp.wait_ge(*low_done(q - RING))
                e, half = q // QPE, q % 2
                if q % QPE < 2:
                    src = w1[e, P * half:P * half + P, :]
                    dst = stage[:, q % RING, :]
                else:
                    src = w2[e, HID // 2 * half:HID // 2 * (half + 1), :].rearrange("(c p) n -> p c n", p=P)
                    dst = stage[:, q % RING, :].rearrange("p (c n) -> p c n", n=D)
                sp.dma_start(dst, src).then_inc(in_w[q % RING], 16)
            sp.wait_ge(used_ready, 1)
            jl, odd = last_pair(sp), odd_blocks(sp)
            sp.wait_ge(scattered[0], 16 * jl + 16)
            sp.wait_ge(scattered[1], 16 * odd)
            sp.dma_start(cb[0:N_EXP, :], y_table[ZERO_TOKEN:ZERO_TOKEN + N_EXP, :]).then_inc(in_cb, 16)
            for q in range(T // 2):
                for k in range(TOPK):
                    r0 = 1 + k * SECOND + 2 * q * P
                    sp.dma_start(y_in[:, k * T + 2 * q:k * T + 2 * q + 2, :],
                                 y_table[r0:r0 + 2 * P, :].rearrange("(t p) n -> p t n", p=P)
                                 ).then_inc(in_y[k][q], 16)
            for q in range(T // 2):
                sp.wait_ge(out_ready, 2 * q + 2)
                sp.dma_start(out.rearrange("b (j p) n -> p (b j) n", p=P)[:, 2 * q:2 * q + 2, :],
                             y_in[:, 2 * q:2 * q + 2, :]).then_inc(out_sent, 16)
            sp.wait_ge(out_sent, 16 * (T // 2))

        @block.gpsimd
        def _(pool):
            def lows(a, b):
                for q in range(a, b):
                    if by_dve(q):
                        continue
                    pool.wait_ge(hi_ready, q + 1)
                    nc.gpsimd.tensor_tensor(out=w_lo[:, q, :], in0=stage[:, q % RING, :], in1=w_hi[:, q, :],
                                            op=ALU.subtract).then_inc(lo_pool, 1)

            wait = pool.wait_ge

            def hold():
                nc.gpsimd.tensor_tensor(out=held[:, :], in0=cst[:, 0:1], in1=cst[:, 0:1], op=ALU.add)

            def gather(j, u):
                s = xg_slot(j, u)
                nc.gpsimd.tensor_copy(gcol[:, s:s + 1], gidx[:, bass.ds(2 * j + u, 1)]).then_inc(gcol_ready, 1)
                wait(gcol_ready, 2 * j + u + 1)
                hold()
                nc.gpsimd.indirect_dma_start(
                    out=xg[:, s, :], out_offset=None, in_=x_table,
                    in_offset=bass.IndirectOffsetOnAxis(ap=gcol[:, s:s + 1], axis=0)).then_inc(gathered[s], 16)

            def scatter(j, u):
                nc.gpsimd.tensor_copy(ycol[:, u:u + 1], yidx[:, bass.ds(2 * j + u, 1)]).then_inc(ycol_ready, 1)
                wait(ycol_ready, 2 * j + u + 1)
                wait(y_ready, 2 * j + u + 1)
                hold()
                nc.gpsimd.indirect_dma_start(
                    out=y_table, out_offset=bass.IndirectOffsetOnAxis(ap=ycol[:, u:u + 1], axis=0),
                    in_=ysb[:, u, :], in_offset=None, bounds_check=ROWS_Y - 1,
                    oob_is_err=False).then_inc(scattered[u], 16)

            lows(0, LATE)
            pool.wait_ge(index_ready, 1)
            pool.wait_ge(in_cst, 16)
            pool.wait_ge(zero_sent, 32)
            for u in range(2):
                pool.wait_ge(table_sent[u], 32)
            for j in range(2):
                for u in range(2):
                    gather(j, u)
            lows(LATE, QUARTERS)

            def pair(j, first=False, last=False):
                if first:
                    for u in range(2):
                        wait(tr_x, u + 1)
                        wait(gathered[u], 16)
                        gather(2, u)
                elif not second(j) and not last:
                    for u in range(2):
                        wait(tr_x, 2 * j + u + 1)
                        wait(gathered[u], 16 * j)
                        gather(j + 1, u)
                if first:
                    wait(index_ready, 2)
                else:
                    if not isinstance(j, int) or j > 1:
                        wait(scattered[1], 16 * (j - 1))
                    scatter(j - 1, 1)
                    wait(scattered[0], 16 * j)
                scatter(j, 0)

            pair(0, first=True)
            pair(1)
            pool.wait_ge(used_ready, 1)
            jl, used = last_pair(pool), used_blocks(pool)
            with pool.Fori(2, JN - 1) as j:
                with pool.If(j < jl):
                    pair(j)
            pair(jl, last=True)
            with pool.If(2 * jl + 1 < used):
                wait(scattered[1], 16 * jl)
                scatter(jl, 1)

        @block.scalar
        def _(act):
            act.dma_start(wqk[:, 0, :], Wq).then_inc(in_wqk, 16)
            act.dma_start(wqk[:, 1, :], Wk).then_inc(in_wqk, 16)
            act.dma_start(bqk[:, 0:1], bq.rearrange("(p a) -> p a", a=1)).then_inc(in_wqk, 16)
            act.dma_start(bqk[:, 1:2], bk.rearrange("(p a) -> p a", a=1)).then_inc(in_wqk, 16)
            act.dma_start(gate[:, 0:1], g_x.rearrange("(o a) -> o a", a=1).broadcast_to([P, 1])).then_inc(in_gate, 16)
            act.dma_start(gate[:, 1:2], g_f.rearrange("(o a) -> o a", a=1).broadcast_to([P, 1])).then_inc(in_gate, 16)

            def high(a, b):
                for q in range(a, b):
                    act.wait_ge(in_w[q % RING], 16 * (q // RING + 1))
                    nc.scalar.activation(w_hi[:, q, :], stage[:, q % RING, :], ACT.Copy).then_inc(hi_ready, 1)

            def stds(n):
                act.wait_ge(var_ready, n)
                nc.scalar.activation(rstd[:, :], rstd[:, :], ACT.Sqrt).then_inc(std_ready, 1)

            act.wait_ge(zero_ready, 1)
            act.dma_start(x_table[0:1, :], zrow[0:1, :]).then_inc(zero_sent, 16)
            act.dma_start(x_table[ZERO_TOKEN:ROWS_X, :], zrow).then_inc(zero_sent, 16)
            nc.scalar.activation(warm[0:1, :], zrow[0:1, 0:1], ACT.Sqrt)
            act.wait_ge(tr_ctx, 2)
            nc.scalar.activation(cfT[:, 512:1024], bank[2][:, :], ACT.Copy).then_inc(ctxT_a, 1)
            for h in range(2):
                act.wait_ge(q_done, h + 1)
                nc.scalar.activation(qT[:, 512 * h:512 * h + 512], bank[3 + h][:, :], ACT.Identity,
                                     bias=bqk[:, 0:1]).then_inc(q_ready, 1)
                act.wait_ge(k_done, h + 1)
                nc.scalar.activation(kT[:, 512 * h:512 * h + 512], bank[5 + h][:, :], ACT.Identity,
                                     bias=bqk[:, 1:2]).then_inc(k_ready, 1)
                if h == 0:
                    high(0, 1)
            stds(1)
            act.wait_ge(in_gate, 32)
            nc.scalar.activation(tg[:, :], gate[:, :], ACT.Tanh).then_inc(tg_ready, 1)
            e_bank = [1, 2, 0, 7]

            def exps(b):
                act.wait_ge(max_ready, b + 1)
                if b >= 2:
                    act.wait_ge(tr_p, b - 1)
                for j in range(2):
                    nc.scalar.activation(prob[:, b % 2, j, :], bank[e_bank[b]][:, L * j:L * j + L], ACT.Exp,
                                         bias=nmax[:, 2 * b + j:2 * b + j + 1],
                                         accum_out=rsum[:, 2 * b + j:2 * b + j + 1]).then_inc(exp_ready, 1)

            def probT_copy(b):
                act.wait_ge(tr_p, b + 1)
                if b >= 2:
                    act.wait_ge(mixed, b - 1)
                nc.scalar.activation(probT[:, b % 2, :, :], bank[e_bank[b]][:, :].rearrange("p (c n) -> p c n", c=2),
                                     ACT.Copy).then_inc(probT_ready, 1)

            exps(0)
            exps(1)
            high(1, 2)
            probT_copy(0)
            exps(2)
            high(2, 4)
            probT_copy(1)
            exps(3)
            high(4, 6)
            probT_copy(2)
            high(6, 8)
            probT_copy(3)
            high(8, 13)
            stds(2)
            high(13, 15)
            high(15, 16)

            def xnT_copy(b):
                act.wait_ge(tr_xn, b + 1)
                if b >= 2:
                    act.wait_ge(rh_done, b - 1)
                nc.scalar.activation(xnT[:, b % 2, :, :], bank[e_bank[b]][:, :].rearrange("p (c n) -> p c n", c=2),
                                     ACT.Copy).then_inc(xnT_ready, 1)

            def router_gelu(b):
                act.wait_ge(rh_done, b + 1)
                if b >= 2:
                    act.wait_ge(logits, b - 1)
                nc.scalar.activation(rh[:, b % 2, :], bank[3 + b][:, 0:L], ACT.Gelu).then_inc(rh_ready, 1)

            def send(b):
                act.wait_ge(split_ready, b + 1)
                act.dma_start(x_table[1 + L * b:1 + L * b + L, :].rearrange("(j p) n -> p j n", p=P),
                              split[b][:, :, :]).then_inc(table_sent[b % 2], 16)

            xnT_copy(0)
            xnT_copy(1)
            router_gelu(0)
            high(16, 17)
            xnT_copy(2)
            router_gelu(1)
            high(17, 18)
            xnT_copy(3)
            high(18, 19)
            router_gelu(2)
            send(0)
            send(1)
            router_gelu(3)
            send(2)
            send(3)
            high(19, 28)
            act.wait_ge(dlg_ready, 1)
            nc.scalar.activation(elg[:, :, :], dlg[:, :, :], ACT.Exp).then_inc(elg_ready, 1)
            high(28, QUARTERS)
            nc.scalar.activation(warm[:, :], tg[:, 0:1], ACT.Gelu)

            act.wait_ge(index_ready, 2)
            act.wait_ge(used_ready, 1)
            jl, used = last_pair(act), used_blocks(act)

            def gelus(j, u):
                i = 2 * j + u
                e = act.value_load(eb[0:1, bass.ds(i, 1)], min_val=0, max_val=N_EXP - 1)
                if not isinstance(j, int) or j:
                    act.wait_ge(h_ready, 4 * i - 4)
                for half in range(2):
                    act.wait_ge(h_done, 2 * i + half + 1)
                    for c in range(4):
                        cc = 4 * half + c
                        last = nc.scalar.activation(hidden[u][:, cc * P:cc * P + P],
                                                    bank[(0 if u == 0 else 6) + half][:, c * P:c * P + P],
                                                    ACT.Gelu, bias=b1T[:, bass.ds(e * HC + cc, 1)])
                    last.then_inc(gelu_done, 1)

            for u in range(2):
                gelus(0, u)
            with act.Fori(1, JN - 1) as j:
                with act.If(j < jl):
                    for u in range(2):
                        gelus(j, u)
            gelus(jl, 0)
            with act.If(2 * jl + 1 < used):
                gelus(jl, 1)

        @block.vector
        def _(dve):
            steps = [0]

            def step(ins):
                steps[0] += 1
                ins.then_inc(v_step, 1)
                dve.wait_ge(v_step, steps[0])

            def low(q):
                dve.wait_ge(hi_ready, q + 1)
                nc.vector.tensor_tensor(out=w_lo[:, q, :], in0=stage[:, q % RING, :], in1=w_hi[:, q, :],
                                        op=ALU.subtract).then_inc(lo_dve, 1)

            def stats(t0, t1):
                for t in range(t0, t1):
                    last = nc.vector.bn_stats(bns[:, t, :], xs[:, t, :])
                return last

            def aggregates(t0, t1, last):
                step(last)
                for t in range(t0, t1):
                    last = nc.vector.bn_aggr(mv[:, t, :], bns[:, t, :])
                step(last)

            def variances():
                nc.vector.tensor_scalar(rstd[:, :], mv[:, :, 1], EPS, None, ALU.add).then_inc(var_ready, 1)

            def inverse(n):
                dve.wait_ge(std_ready, n)
                step(nc.vector.reciprocal(rstd[:, :], rstd[:, :]))

            def normalise(t0, t1, ready):
                for t in range(t0, t1):
                    nc.vector.tensor_scalar(lnx[:, t, :], xs[:, t, :], mv[:, t, 0:1], rstd[:, t:t + 1],
                                            ALU.subtract, ALU.mult).then_inc(ready, 1)

            nc.vector.memset(zrow, 0.0).then_inc(zero_ready, 1)
            nc.vector.memset(filler, 1.0).then_inc(zero_ready, 1)
            dve.wait_ge(tr_w, 1)
            nc.vector.tensor_copy(wqkT[:, :, :], bank[0][:, 0:2 * C].rearrange("p (a n) -> p a n", a=2)).then_inc(wT_ready, 1)
            dve.wait_ge(tr_ctx, 1)
            nc.vector.tensor_copy(cfT[:, 0:512], bank[1][:, :]).then_inc(ctxT_v, 1)
            dve.wait_ge(tr_w, 2)
            nc.vector.tensor_copy(b1T[:, :], bank[7][:, 0:HC * N_EXP]).then_inc(wT_ready, 1)
            dve.wait_ge(in_x, 16)
            aggregates(0, T, stats(0, T))
            variances()
            e_bank = [1, 2, 0, 7]

            def maxima(b):
                dve.wait_ge(energy, b + 1)
                nc.vector.tensor_reduce(out=nmax[:, 2 * b:2 * b + 2],
                                        in_=bank[e_bank[b]][:, :].rearrange("p (j n) -> p j n", j=2),
                                        axis=X, op=ALU.max, negate=True).then_inc(max_ready, 1)

            def probs(b):
                dve.wait_ge(exp_ready, 2 * b + 2)
                step(nc.vector.reciprocal(rinv[:, 2 * b:2 * b + 2], rsum[:, 2 * b:2 * b + 2]))
                for j in range(2):
                    last = nc.vector.tensor_scalar(prob[:, b % 2, j, :], prob[:, b % 2, j, :],
                                                   rinv[:, 2 * b + j:2 * b + j + 1], None, ALU.mult)
                last.then_inc(prob_ready, 1)

            def lnT_copy(b):
                dve.wait_ge(tr_ln, b + 1)
                if b >= 2:
                    dve.wait_ge(mixed, b - 1)
                nc.vector.tensor_copy(lnT[:, b % 2, :, :], bank[3 + b][:, :].rearrange("p (c n) -> p c n", c=2)
                                      ).then_inc(lnT_ready, 1)

            def residual(b):
                dve.wait_ge(mixed, b + 1)
                if b == 0:
                    dve.wait_ge(tg_ready, 1)
                nc.vector.scalar_tensor_tensor(out=xs[:, 2 * b:2 * b + 2, :],
                                               in0=bank[3 + b][:, :].rearrange("p (j n) -> p j n", j=2),
                                               scalar=tg[:, 0:1], in1=xs[:, 2 * b:2 * b + 2, :],
                                               op0=ALU.mult, op1=ALU.add).then_inc(x2_ready, 1)

            def stats_of(b):
                dve.wait_ge(x2_ready, b + 1)
                return stats(2 * b, 2 * b + 2)

            inverse(1)
            normalise(0, 2, ln_ready)
            maxima(0)
            maxima(1)
            normalise(2, 4, ln_ready)
            probs(0)
            dve.wait_ge(zero_sent, 32)
            lnT_copy(0)
            maxima(2)
            normalise(4, 6, ln_ready)
            probs(1)
            lnT_copy(1)
            maxima(3)
            normalise(6, T, ln_ready)
            low(3)
            residual(0)
            probs(2)
            lnT_copy(2)
            residual(1)
            probs(3)
            lnT_copy(3)
            low(7)
            stats_of(0)
            residual(2)
            stats_of(1)
            aggregates(0, 6, stats_of(2))
            low(11)
            residual(3)
            aggregates(6, T, stats_of(3))
            variances()
            inverse(2)
            normalise(0, T, xn_ready)
            for b in range(B):
                dve.wait_ge(xn_ready, 2 * b + 2)
                if b == 0:
                    dve.wait_ge(mixed, B)
                hi_p, lo_p = split[b][:, :, 0:D], split[b][:, :, D:2 * D].bitcast(BF16)
                step(nc.vector.tensor_copy(hi_p, lnx[:, 2 * b:2 * b + 2, :]))
                nc.vector.tensor_tensor(out=lo_p, in0=lnx[:, 2 * b:2 * b + 2, :], in1=hi_p,
                                        op=ALU.subtract).then_inc(split_ready, 1)
                if b == 0:
                    low(15)
            nc.vector.tensor_copy(ident16[:, :], ident)
            nc.vector.tensor_copy(identb[:, :], ident)
            nc.vector.tensor_copy(upper16[:, :], cst[:, C_UP:C_UP + P])
            nc.vector.tensor_copy(iota16[:, :], cst[:, C_IOTA:C_IOTA + P])
            nc.vector.memset(ones16[:, :], 1.0)
            nc.vector.memset(M16[:, 0:T - 1, :], 0.0)
            nc.vector.tensor_scalar(col0[:, :], cst[:, C_IOTA:C_IOTA + P], 0.0, None,
                                    ALU.is_equal).then_inc(small_ready, 1)

            low(18)

            def e_bc(ap):
                return ap.unsqueeze(1).broadcast_to(te)

            def t_bc(ap):
                return ap.unsqueeze(2).broadcast_to(te)

            dve.wait_ge(logits, B)
            lg = bank[1][:, 0:T * N_EXP].rearrange("p (t e) -> p t e", t=T)
            for k in range(TOPK):
                src = lg if k == 0 else lg2
                step(nc.vector.tensor_reduce(out=top[:, k, :], in_=src, axis=X, op=ALU.max))
                step(nc.vector.tensor_tensor(out=sc, in0=src, in1=t_bc(top[:, k, :]), op=ALU.is_equal))
                step(nc.vector.tensor_tensor(out=sc, in0=sc, in1=e_bc(desc), op=ALU.mult))
                step(nc.vector.tensor_reduce(out=pick[:, k, :], in_=sc, axis=X, op=ALU.max))
                step(nc.vector.tensor_tensor(out=E16[:, k, :, :], in0=e_bc(desc), in1=t_bc(pick[:, k, :]), op=ALU.is_equal))
                if k == 0:
                    step(nc.vector.scalar_tensor_tensor(out=lg2, in0=E16[:, 0, :, :], scalar=-BIG,
                                                        in1=lg, op0=ALU.mult, op1=ALU.add))
            nc.vector.tensor_tensor(out=M16[:, T - 1:2 * T - 1, :], in0=E16[:, 0, :, :], in1=E16[:, 1, :, :],
                                    op=ALU.add).then_inc(choice_ready, 1)
            nc.vector.tensor_tensor(out=dlg[:, :, :], in0=lg, in1=t_bc(top[:, 0, :]),
                                    op=ALU.subtract).then_inc(dlg_ready, 1)
            dve.wait_ge(counted, 1)
            step(nc.vector.tensor_reduce(out=nexp[:, :], in_=bank[2][:, 2 * P:2 * P + T * N_EXP].rearrange(
                "p (t e) -> p e t", t=T), axis=X, op=ALU.add))
            ee = [P, N_EXP, N_EXP]
            eth = [P, N_EXP, N_EXP + 1]
            step(nc.vector.tensor_tensor(out=ge[:, :, :], in0=nexp[:, :].unsqueeze(2).broadcast_to(eth),
                                         in1=thr.unsqueeze(1).broadcast_to(eth), op=ALU.is_ge))
            step(nc.vector.tensor_reduce(out=cnt[:, :], in_=ge[:, :, :], axis=X, op=ALU.add))
            step(nc.vector.tensor_tensor(out=ltc[:, :, :], in0=lt, in1=cnt[:, :].unsqueeze(1).broadcast_to(ee), op=ALU.mult))
            step(nc.vector.tensor_reduce(out=st_[:, :], in_=ltc[:, :, :], axis=X, op=ALU.add))
            step(nc.vector.tensor_tensor(out=slotb, in0=bank[2][:, 0:T * N_EXP].rearrange("p (t e) -> p t e", t=T),
                                         in1=e_bc(st_[:, :]), op=ALU.add))
            kte = [P, TOPK, T * N_EXP]
            e2 = E16[:, :, :, :].rearrange("p k t e -> p k (t e)")
            sp2 = sprod.rearrange("p k t e -> p k (t e)")
            step(nc.vector.tensor_tensor(out=sp2, in0=e2,
                                         in1=slotb.rearrange("p t e -> p (t e)").unsqueeze(1).broadcast_to(kte),
                                         op=ALU.mult))
            step(nc.vector.tensor_reduce(out=slot_f[:, :], in_=sprod.rearrange("p k t e -> p (k t) e"),
                                         axis=X, op=ALU.add))
            step(nc.vector.tensor_copy(slot[:, :], slot_f[:, :]))
            nc.vector.tensor_scalar(blk_i[:, :], slot[:, :], SLOTS - P, None, ALU.bitwise_and)
            step(nc.vector.tensor_scalar(r_i[:, :], slot[:, :], P - 1, None, ALU.bitwise_and))
            nc.vector.tensor_copy(blk_f[:, :], blk_i[:, :])
            step(nc.vector.tensor_copy(r_f[:, :], r_i[:, :]))
            kb = [P, TOPK * T, BLOCKS]
            step(nc.vector.tensor_tensor(out=ohb[:, :, :], in0=iota_b.unsqueeze(1).broadcast_to(kb),
                                         in1=blk_f[:, :].unsqueeze(2).broadcast_to(kb), op=ALU.is_equal))
            step(nc.vector.tensor_tensor(out=ltc[:, 0, :], in0=st_[:, :], in1=cst[:, C_ID:C_ID + N_EXP], op=ALU.mult))
            step(nc.vector.tensor_reduce(out=scol[:, :], in_=ltc[:, 0, :], axis=X, op=ALU.add))
            nc.vector.tensor_scalar(dumb[:, :], iota_b, scol[:, :], dcode, ALU.is_equal, ALU.mult)
            for kt in range(TOPK * T):
                last = nc.vector.tensor_scalar(ohr[:, kt, :], iota16[:, :], r_f[:, kt:kt + 1],
                                               tokp1[:, kt % T:kt % T + 1], ALU.is_equal, ALU.mult)
                last.then_inc(onehot_ready, 1)
            step(nc.vector.scalar_tensor_tensor(out=en[:, :], in0=cnt[:, :], scalar=float(P), in1=st_[:, :],
                                                op0=ALU.mult, op1=ALU.add))
            be = [P, BLOCKS, N_EXP]
            step(nc.vector.tensor_tensor(out=ebge, in0=iota_b.unsqueeze(2).broadcast_to(be),
                                         in1=en[:, :].unsqueeze(1).broadcast_to(be), op=ALU.is_ge))
            step(nc.vector.tensor_reduce(out=ebf[:, :], in_=ebge, axis=X, op=ALU.add))
            nc.vector.tensor_scalar(eb[:, :], ebf[:, :], float(N_EXP - 1), None, ALU.min)
            dve.wait_ge(codes_done, 1)
            code = bank[0][:, 0:BLOCKS]
            nc.vector.tensor_copy(gidx[:, :], code).then_inc(index_ready, 1)
            nc.vector.tensor_reduce(out=tot[:, :, :],
                                         in_=bank[2][:, P:2 * P].rearrange("p (k t e) -> p k e t", k=TOPK, t=T),
                                         axis=X, op=ALU.add)


            step(nc.vector.tensor_scalar(yt1[:, :], code, 0.0, float(SKIP), ALU.is_equal, ALU.mult))
            step(nc.vector.tensor_tensor(out=yt2[:, :], in0=yt1[:, :], in1=code, op=ALU.add))
            step(nc.vector.tensor_scalar(yt1[:, :], bank[0][:, BLOCKS:2 * BLOCKS], 0.0, float(SECOND),
                                         ALU.is_gt, ALU.mult))
            nc.vector.tensor_tensor(out=yidx[:, :], in0=yt1[:, :], in1=yt2[:, :], op=ALU.add).then_inc(index_ready, 1)
            def xT_copy(j, u):
                i = 2 * j + u
                dve.wait_ge(tr_x, i + 1)
                if not isinstance(j, int) or j:
                    dve.wait_ge(h_done, 2 * i - 2)
                nc.vector.tensor_copy(xT[:, u, :].bitcast(I32),
                                      bank[2 + u][:, 0:D].bitcast(I32)).then_inc(xT_ready, 1)

            def hidden_split(j, u, half):
                i = 2 * j + u
                if half == 0 and (not isinstance(j, int) or j):
                    dve.wait_ge(y_done, i - 1)
                dve.wait_ge(gelu_done, 2 * i + half + 1)
                hs = hidden[u][:, 512 * half:512 * half + 512].rearrange("p (c n) -> p c n", n=P)
                hh, hl = h_hi[:, u, 4 * half:4 * half + 4, :], h_lo[:, u, 4 * half:4 * half + 4, :]
                nc.vector.tensor_copy(hh, hs).then_inc(h_ready, 1)
                dve.wait_ge(h_ready, 4 * i + 2 * half + 1)
                nc.vector.tensor_tensor(out=hl, in0=hs, in1=hh, op=ALU.subtract).then_inc(h_ready, 1)

            def y_copy(j, u):
                i = 2 * j + u
                dve.wait_ge(y_done, i + 1)
                if not isinstance(j, int) or j:
                    dve.wait_ge(scattered[u], 16 * j)
                nc.vector.tensor_copy(ysb[:, u, :], bank[4 + u][:, 0:D]).then_inc(y_ready, 1)

            def fetch_w1(i, u):
                e = dve.value_load(eb[0:1, bass.ds(i, 1)], min_val=0, max_val=N_EXP - 1)
                if not isinstance(i, int) or i > 3:
                    dve.wait_ge(h_done, 2 * i - 2)
                for h in range(2):
                    nc.vector.tensor_copy(w1f[:, u, h, :].bitcast(I32).unsqueeze(1),
                                          w1_words[h][:, bass.ds(e, 1), 0:QW]).then_inc(w1_fetched, 1)

            low(25)
            low(27)
            low(28)
            used = ((0, P + LEAST_LAST * 2 * P, 2 * P), (1, LEAST_ODD * 2 * P, 2 * P), (2, LEAST * P, P))
            for n, least, size in used:
                last = nc.vector.tensor_scalar(used_f[:, n:n + 1], en[:, N_EXP - 1:N_EXP], float(least), None,
                                               ALU.subtract)
            step(last)
            step(nc.vector.tensor_copy(used_i[:, :], used_f[:, :]))
            for n, least, size in used:
                last = nc.vector.tensor_scalar(used_i[:, n:n + 1], used_i[:, n:n + 1], size.bit_length() - 1, None,
                                               ALU.logical_shift_right)
            last.then_inc(used_ready, 1)
            xT_copy(0, 0)
            low(30)
            dve.wait_ge(elg_ready, 1)
            step(nc.vector.tensor_reduce(out=z[:, :], in_=elg[:, :, :], axis=X, op=ALU.add))
            step(nc.vector.reciprocal(z[:, :], z[:, :]))
            step(nc.vector.tensor_tensor(out=sp2, in0=e2,
                                         in1=elg[:, :, :].rearrange("p t e -> p (t e)").unsqueeze(1).broadcast_to(kte),
                                         op=ALU.mult))
            step(nc.vector.tensor_reduce(out=wk[:, :, :], in_=sprod, axis=X, op=ALU.add))
            step(nc.vector.scalar_tensor_tensor(out=wk[:, :, :], in0=wk[:, :, :], scalar=tg[:, 1:2],
                                                in1=z[:, :].unsqueeze(1).broadcast_to([P, TOPK, T]),
                                                op0=ALU.mult, op1=ALU.mult))
            xT_copy(0, 1)
            hidden_split(0, 0, 0)
            xT_copy(1, 0)
            hidden_split(0, 0, 1)
            wait_weights(dve, QUARTERS - 5)
            fetch_w1(2, 0)
            hidden_split(0, 1, 0)
            step(nc.vector.tensor_scalar(act_f[:, :, :], tot[:, :, :], 0.0, None, ALU.is_gt))
            for k in range(TOPK):
                step(nc.vector.tensor_tensor(out=dcat[:, k, :, :], in0=e_bc(act_f[:, k, :]), in1=E16[:, k, :, :],
                                             op=ALU.subtract))
                step(nc.vector.tensor_tensor(out=dcat[:, k, :, :], in0=dcat[:, k, :, :], in1=t_bc(wk[:, k, :]),
                                             op=ALU.mult))
                step(nc.vector.tensor_tensor(out=sprod[:, k, :, :], in0=e_bc(act_f[:, k, :]), in1=t_bc(wk[:, k, :]),
                                             op=ALU.mult))
            nc.vector.tensor_tensor(out=cat[:, :, 0:N_EXP], in0=dcat[:, 0, :, :], in1=dcat[:, 1, :, :], op=ALU.add)
            step(nc.vector.tensor_tensor(out=cat[:, :, N_EXP:2 * N_EXP], in0=sprod[:, 0, :, :], in1=sprod[:, 1, :, :],
                                         op=ALU.add))
            y_copy(0, 0)

            def pair(j):
                xT_copy(j, 1)
                hidden_split(j - 1, 1, 1)
                fetch_w1(2 * j + 1, 1)
                hidden_split(j, 0, 0)
                y_copy(j - 1, 1)
                xT_copy(j + 1, 0)
                hidden_split(j, 0, 1)
                fetch_w1(2 * j + 2, 0)
                hidden_split(j, 1, 0)
                y_copy(j, 0)

            wait_weights(dve, QUARTERS - 3)
            pair(1)
            wait_weights(dve, QUARTERS - 1)
            dve.wait_ge(used_ready, 1)
            jl, used = last_pair(dve), used_blocks(dve)
            with dve.Fori(2, JN - 1) as j:
                with dve.If(j < jl):
                    pair(j)
            xT_copy(jl, 1)
            hidden_split(jl - 1, 1, 1)
            fetch_w1(2 * jl + 1, 1)
            hidden_split(jl, 0, 0)
            y_copy(jl - 1, 1)
            hidden_split(jl, 0, 1)
            with dve.If(2 * jl + 1 < used):
                hidden_split(jl, 1, 0)
            y_copy(jl, 0)
            with dve.If(2 * jl + 1 < used):
                hidden_split(jl, 1, 1)
                y_copy(jl, 1)

            dve.wait_ge(tr_cat, 1)
            for half in range(2):
                nc.vector.tensor_copy(catT[:, 512 * half:512 * half + 512],
                                      bank[half][0:2 * N_EXP, :]).then_inc(catT_ready, 1)
            for q in range(T // 2):
                dve.wait_ge(in_y[0][q], 16)
                dve.wait_ge(const_done, q + 1)
                for t in (2 * q, 2 * q + 1):
                    last = nc.vector.scalar_tensor_tensor(
                        out=y_in[:, t, :], in0=y_in[:, t, :], scalar=wk[:, 0, t:t + 1],
                        in1=bank[(2, 3, 6, 7)[q]][:, (t % 2) * D:(t % 2 + 1) * D], op0=ALU.mult, op1=ALU.add)
                step(last)
                dve.wait_ge(in_y[1][q], 16)
                for t in (2 * q, 2 * q + 1):
                    nc.vector.scalar_tensor_tensor(
                        out=y_in[:, t, :], in0=y_in[:, T + t, :], scalar=wk[:, 1, t:t + 1],
                        in1=y_in[:, t, :], op0=ALU.mult, op1=ALU.add).then_inc(out_ready, 1)

        @block.tensor
        def _(pe):
            mm, tr = nc.tensor.matmul, nc.tensor.transpose
            e_bank = [1, 2, 0, 7]

            def keep_busy(n, b, data):
                for _ in range(n):
                    mm(bank[b][:, :], data[:, 0:P], data, start=True, stop=True)

            pe.wait_ge(zero_ready, 2)
            keep_busy(11, 0, filler)
            pe.wait_ge(in_cst, 16)
            pe.wait_ge(in_wqk, 64)
            for a in range(2):
                last = tr(bank[0][:, C * a:C * a + C], wqk[:, a, :], ident)
            last.then_inc(tr_w, 1)
            pe.wait_ge(in_ctx, 16)
            for h in range(2):
                for t in range(4):
                    last = tr(bank[1 + h][:, P * t:P * t + P], cf[:, 4 * h + t, :], ident)
                last.then_inc(tr_ctx, 1)
            pe.wait_ge(in_bias, 32)
            tr(bank[7][:, 0:HC * N_EXP], b1r, cst[0:HC * N_EXP, C_ID:C_ID + HC * N_EXP]).then_inc(tr_w, 1)
            pe.wait_ge(wT_ready, 1)
            for h in range(2):
                if h == 0:
                    pe.wait_ge(ctxT_v, 1)
                else:
                    pe.wait_ge(ctxT_a, 1)
                mm(bank[3 + h][:, :], wqkT[:, 0, :], cfT[:, 512 * h:512 * h + 512], start=True, stop=True).then_inc(q_done, 1)
                mm(bank[5 + h][:, :], wqkT[:, 1, :], cfT[:, 512 * h:512 * h + 512], start=True, stop=True).then_inc(k_done, 1)

            def energies(b):
                pe.wait_ge(q_ready, b // 2 + 1)
                pe.wait_ge(k_ready, b // 2 + 1)
                if b == 3:
                    pe.wait_ge(wT_ready, 2)
                for j in range(2):
                    last = mm(bank[e_bank[b]][:, L * j:L * j + L], qT[:, L * b + P * j:L * b + P * j + P],
                              kT[:, L * b:L * b + L], start=True, stop=True)
                last.then_inc(energy, 1)

            def lnT_tr(b):
                pe.wait_ge(ln_ready, 2 * b + 2)
                pe.wait_ge(q_ready, 2)
                pe.wait_ge(k_ready, 2)
                for c in range(2):
                    for j in range(2):
                        last = tr(bank[3 + b][:, L * c + P * j:L * c + P * j + P], lnx[:, 2 * b + j, P * c:P * c + P], ident)
                last.then_inc(tr_ln, 1)

            def probT_tr(b):
                pe.wait_ge(prob_ready, b + 1)
                for c in range(2):
                    for j in range(2):
                        last = tr(bank[e_bank[b]][:, L * c + P * j:L * c + P * j + P], prob[:, b % 2, j, P * c:P * c + P], ident)
                last.then_inc(tr_p, 1)

            def mix(b):
                pe.wait_ge(lnT_ready, b + 1)
                pe.wait_ge(probT_ready, b + 1)
                for j in range(2):
                    for c in range(2):
                        last = mm(bank[3 + b][:, L * j:L * j + L], lnT[:, b % 2, c, P * j:P * j + P],
                                  probT[:, b % 2, c, :], start=(c == 0), stop=(c == 1))
                last.then_inc(mixed, 1)

            for b in range(B):
                energies(b)
            lnT_tr(0)
            probT_tr(0)
            lnT_tr(1)
            mix(0)
            probT_tr(1)
            lnT_tr(2)
            mix(1)
            probT_tr(2)
            lnT_tr(3)
            mix(2)
            probT_tr(3)
            mix(3)
            pe.wait_ge(in_router, 32)
            keep_busy(24, 1, w_hi[:, 0, 0:512])

            def xnT_tr(b):
                pe.wait_ge(xn_ready, 2 * b + 2)
                for c in range(2):
                    for j in range(2):
                        last = tr(bank[e_bank[b]][:, L * c + P * j:L * c + P * j + P], lnx[:, 2 * b + j, P * c:P * c + P], ident)
                last.then_inc(tr_xn, 1)

            def router_hidden(b):
                pe.wait_ge(xnT_ready, b + 1)
                pe.wait_ge(x2_ready, b + 1)
                for c in range(DC):
                    last = mm(bank[3 + b][:, 0:L], rw1_s[:, c, :], xnT[:, b % 2, c, :], start=(c == 0), stop=(c == DC - 1))
                last.then_inc(rh_done, 1)

            def router_logits(b):
                pe.wait_ge(rh_ready, b + 1)
                for j in range(2):
                    t = 2 * b + j
                    last = mm(bank[1][:, t * N_EXP:(t + 1) * N_EXP], rh[:, b % 2, P * j:P * j + P], rw2_s[:, :],
                              start=True, stop=True)
                last.then_inc(logits, 1)

            xnT_tr(0)
            xnT_tr(1)
            router_hidden(0)
            xnT_tr(2)
            router_hidden(1)
            router_logits(0)
            xnT_tr(3)
            router_hidden(2)
            router_logits(1)
            router_hidden(3)
            router_logits(2)
            router_logits(3)

            pe.wait_ge(small_ready, 1)
            pe.wait_ge(choice_ready, 1)
            n = T * N_EXP
            m2 = M16[:, :, :].rearrange("p t e -> p (t e)")
            mm(bank[2][:, 2 * P:2 * P + n], ones16[:, :], m2[:, (T - 1) * N_EXP:(2 * T - 1) * N_EXP], start=True, stop=True)
            mm(bank[2][:, P:2 * P], ones16[:, :], E16[:, :, :, :].rearrange("p k t e -> p (k t e)"), start=True, stop=True)
            mm(bank[2][:, 0:n], upper16[:, :], m2[:, (T - 1) * N_EXP:(2 * T - 1) * N_EXP], start=True, stop=False)
            for s in range(1, T):
                last = mm(bank[2][:, 0:n], ones16[:, :], m2[:, (T - 1 - s) * N_EXP:(2 * T - 1 - s) * N_EXP],
                          start=False, stop=(s == T - 1))
            last.then_inc(counted, 1)
            pe.wait_ge(onehot_ready, 1)
            mm(bank[0][:, 0:BLOCKS], col0[:, :], dumb[:, :], start=True, stop=False)
            for kt in range(TOPK * T):
                pe.wait_ge(onehot_ready, kt + 1)
                mm(bank[0][:, 0:BLOCKS], ohr[:, kt, :], ohb[:, kt, :], start=False, stop=(kt == TOPK * T - 1))
            for kt in range(T, TOPK * T):
                last = mm(bank[0][:, BLOCKS:2 * BLOCKS], ohr[:, kt, :], ohb[:, kt, :], start=(kt == T),
                          stop=(kt == TOPK * T - 1))
            last.then_inc(codes_done, 1)
            keep_busy(11, 7, w_hi[:, 0, 0:512])
            pe.wait_ge(index_ready, 2)

            def tokens_tr(j, u):
                s = xg_slot(j, u)
                pe.wait_ge(*tokens_in(j, u))
                for c in range(2 * DC):
                    if c < DC:
                        last = tr(bank[2 + u][:, :].bitcast(F16)[:, P * c:P * c + P], xg[:, s, P * c:P * c + P], ident16[:, :])
                    else:
                        last = tr(bank[2 + u][:, :].bitcast(BF16)[:, P * c:P * c + P],
                                  xg[:, s, P * c:P * c + P].bitcast(BF16), identb[:, :])
                last.then_inc(tr_x, 1)

            def expert_of(i):
                return pe.value_load(eb[0:1, bass.ds(i, 1)], min_val=0, max_val=N_EXP - 1)

            experts = [pe.alloc_register(f"expert_{n}") for n in ("before", "even")]

            def load_experts(j):
                for k, r in enumerate(experts):
                    pe.load(r, eb[0:1, bass.ds(2 * j - 1 + k, 1)])

            def up(i, u, e, c):
                if c == 0:
                    pe.wait_ge(xT_ready, i + 1)
                    if e is None:
                        pe.wait_ge(w1_fetched, 2 * i - 2)
                xh = xT[:, u, 0:D].rearrange("p (d n) -> p d n", d=DC)
                xl = xT[:, u, D:2 * D].bitcast(BF16).rearrange("p (d n) -> p d n", d=DC)
                o = bank[(0 if u == 0 else 6) + c // 4][:, (c % 4) * P:(c % 4 + 1) * P]
                cs = slice(c * P, (c + 1) * P)
                for d in range(DC):
                    if e is None:
                        wh, wl = w1f_hi[u][:, d, cs], w1f_lo[u][:, d, cs]
                    else:
                        wh, wl = w1_hi[:, bass.ds(e, 1), d, cs], w1_lo[:, bass.ds(e, 1), d, cs]
                    mm(o, wh, xh[:, d, :], start=(d == 0), stop=False)
                    mm(o, wh, xl[:, d, :], start=False, stop=False)
                    last = mm(o, wl, xh[:, d, :], start=False, stop=(d == DC - 1))
                if c % 4 == 3:
                    last.then_inc(h_done, 1)

            def down(i, u, e, c):
                if c % 4 == 0:
                    pe.wait_ge(h_ready, 4 * i + c // 2 + 2)
                o = bank[4 + u][:, 0:D]
                mm(o, h_hi[:, u, c, :], w2_hi[:, bass.ds(e, 1), 1, c, :], start=(c == 0), stop=False)
                mm(o, h_hi[:, u, c, :], w2_lo[:, bass.ds(e, 1), 1, c, :], start=False, stop=False)
                last = mm(o, h_lo[:, u, c, :], w2_hi[:, bass.ds(e, 1), 1, c, :], start=False, stop=(c == HC - 1))
                if c == HC - 1:
                    last.then_inc(y_done, 1)

            tokens_tr(0, 0)
            wait_weights(pe, QPE - 1)
            for c in range(HC):
                up(0, 0, 0, c)
            tokens_tr(0, 1)
            wait_weights(pe, 2 * QPE - 1)
            tokens_tr(1, 0)
            e1 = expert_of(1)
            for c in range(HC):
                up(1, 1, e1, c)
                down(0, 0, 0, c)
            wait_weights(pe, 4 * QPE - 1)

            def first_half(j):
                ea, eb_ = [pe.snap(r, min_val=0, max_val=N_EXP - 1) for r in experts]
                tokens_tr(j, 1)
                for c in range(HC):
                    up(2 * j, 0, None, c)
                    down(2 * j - 1, 1, ea, c)
                return eb_

            def pair(j):
                i = 2 * j
                eb_ = first_half(j)
                load_experts(j + 1)
                tokens_tr(j + 1, 0)
                for c in range(HC):
                    up(i + 1, 1, None, c)
                    down(i, 0, eb_, c)

            load_experts(1)
            pair(1)
            wait_weights(pe, QUARTERS - 1)
            pe.wait_ge(used_ready, 1)
            jl, used = last_pair(pe), used_blocks(pe)
            with pe.Fori(2, JN - 1) as j:
                with pe.If(j < jl):
                    pair(j)
            eb_ = first_half(jl)

            def residual_to(q):
                mm(bank[(2, 3, 6, 7)[q]][:, :], ident, xs[:, 2 * q:2 * q + 2, :].rearrange("p t n -> p (t n)"),
                   start=True, stop=False)

            with pe.If(2 * jl + 1 < used):
                for c in range(HC):
                    up(2 * jl + 1, 1, None, c)
                    down(2 * jl, 0, eb_, c)
                el = expert_of(2 * jl + 1)
                residual_to(0)
                for c in range(HC):
                    down(2 * jl + 1, 1, el, c)
            with pe.Else():
                residual_to(0)
                for c in range(HC):
                    down(2 * jl, 0, eb_, c)
            pe.wait_ge(gelu_done, 2 * used)
            pe.wait_ge(xT_ready, 2 * jl + 2)
            for t in range(T):
                last = tr(bank[t // 4][0:2 * N_EXP, P * (t % 4):P * (t % 4) + P], cat[:, t, :], ident)
            last.then_inc(tr_cat, 1)
            for q in range(1, T // 2):
                residual_to(q)
            pe.wait_ge(catT_ready, 2)
            pe.wait_ge(in_cb, 16)
            for t in range(T):
                last = mm(bank[(2, 3, 6, 7)[t // 2]][:, (t % 2) * D:(t % 2 + 1) * D], catT[:, P * t:P * t + P],
                          cb[:, :], start=False, stop=(t % 2 == 1))
                if t % 2:
                    last.then_inc(const_done, 1)


_INS = ['x', 'ctx_1024', 'g_xattn', 'g_ffn', 'L0_xattn_Wq', 'L0_xattn_bq', 'L0_xattn_Wk', 'L0_xattn_bk',
        'L0_ffn_rw1', 'L0_ffn_rw2', 'L0_ffn_w1', 'L0_ffn_b1', 'L0_ffn_w2', 'L0_ffn_b2']


def shape_constants():
    import numpy as np
    c = np.zeros((P, C_ALL), np.float32)
    p = np.arange(P)
    c[:, C_ID:C_ID + P] = np.eye(P)
    c[:, C_UP:C_UP + P] = p[:, None] <= p[None, :]
    c[:, C_IOTA:C_IOTA + P] = p[None, :]
    c[:, C_DESC:C_DESC + N_EXP] = N_EXP - np.arange(N_EXP)
    e = np.arange(N_EXP)
    c[:, C_LT:C_LT + N_EXP * N_EXP] = P * (e[None, :] < e[:, None]).reshape(-1)
    c[:, C_THR:C_THR + N_EXP + 1] = P * np.arange(N_EXP + 1)
    c[:, C_BLK:C_BLK + BLOCKS] = P * np.arange(BLOCKS)
    c[:, C_TOK:C_TOK + T] = 1 + p[:, None] + P * np.arange(T)[None, :]
    c[:N_EXP, C_DUM] = ZERO_TOKEN + e
    return c


def kernel(**inputs):
    import numpy as _np
    import concourse.bacc as _bacc
    from concourse import mybir as _mybir
    from concourse.bass_utils import run_bass_kernel_spmd as _run

    nc = _bacc.Bacc("TRN2", target_bir_lowering=False, num_devices=1)
    arrays, args = {}, []
    for name in _INS:
        a = _np.ascontiguousarray(inputs[name])
        arrays[f"in_{name}"] = a
        args.append(nc.dram_tensor(f"in_{name}", a.shape, _mybir.dt.from_np(a.dtype), kind="ExternalInput").ap())
    a = shape_constants()
    arrays["in_consts"] = a
    args.append(nc.dram_tensor("in_consts", a.shape, _mybir.dt.from_np(a.dtype), kind="ExternalInput").ap())
    args.append(nc.dram_tensor("out_0", (B, L, D), _mybir.dt.float32, kind="ExternalOutput").ap())
    flamingo_moe_kernel(nc, *args)
    r = _run(nc, [arrays], core_ids=[0])
    return r.results[0]["out_0"]
```
